# Optimizing a Trainium2 kernel written in Bass

```python
import numpy as np
import jax
import jax.numpy as jnp

def _softmax(x, axis=-1):
    return jax.nn.softmax(x, axis=axis)
def _gelu(x):
    return jax.nn.gelu(x, approximate=True)
def _silu(x):
    return jax.nn.silu(x)
def _sigmoid(x):
    return jax.nn.sigmoid(x)
def _layernorm(x, axis=-1, eps=1e-5):
    m = jnp.mean(x, axis=axis, keepdims=True)
    v = jnp.var(x, axis=axis, keepdims=True)
    return (x - m) / jnp.sqrt(v + eps)
def _scatter_add(tgt, idx, src, axis=0):
    return tgt.at[idx].add(src)
def _segment_sum(src, seg, n):
    return jax.ops.segment_sum(src, seg, n)

kernel_name = 'mk_metaformer_d1_conv_nchw256_7f3487'

def setup_inputs(seed: int = 0):
    np.random.seed(seed)
    _w = jnp.asarray
    def _rec_inputs():
        import jax
        import jax.numpy as jnp
        _gk = jax.random.key(seed)
        x = -0.0006537 + 1.001 * jax.random.normal(jax.random.fold_in(_gk, 1), (1, 256, 96, 96), jnp.float32)
        return x
    x = _rec_inputs()
    def _L0_conv_setup():
        import jax, jax.numpy as jnp
        import numpy as np
        CUTOFF = 0.05

        def _freq_filter(x_chw, filter_type):
            x = jax.lax.stop_gradient(x_chw)
            C, H, W = x.shape
            a = jnp.abs(x)
            mn = a.min(axis=(1, 2), keepdims=True)
            ptp = a.max(axis=(1, 2), keepdims=True) - mn
            q = jnp.floor(255.0 * (a - mn) / ptp)
            f = jnp.fft.fftshift(jnp.fft.fft2(q), axes=(-2, -1))
            crow, ccol = (H // 2, W // 2)
            dr, dc = (int(CUTOFF * crow), int(CUTOFF * ccol))
            m = jnp.zeros((H, W), dtype=q.dtype)
            m = m.at[crow - dr:crow + dr, ccol - dc:ccol + dc].set(1.0)
            if filter_type == 'low_pass':
                m = 1.0 - m
            out = jnp.abs(jnp.fft.ifft2(jnp.fft.ifftshift(f * m, axes=(-2, -1))))
            return out.astype(x_chw.dtype)

        def _conv1x1(x, w, b):
            return jnp.einsum('oc,bchw->bohw', w, x) + b[None, :, None, None]
        key = jax.random.key(seed)
        ks = jax.random.split(key, 7)
        B, C, H, W = (1, 256, 96, 96)
        fuse = jax.random.normal(ks[0], (B, C, H, W), dtype=jnp.float32)
        s = 1.0 / np.sqrt(C)
        Wq = jax.random.normal(ks[1], (C, C), dtype=jnp.float32) * s
        bq = jax.random.normal(ks[2], (C,), dtype=jnp.float32) * 0.01
        Wk = jax.random.normal(ks[3], (C, C), dtype=jnp.float32) * s
        bk = jax.random.normal(ks[4], (C,), dtype=jnp.float32) * 0.01
        Wv = jax.random.normal(ks[5], (C, C), dtype=jnp.float32) * s
        bv = jax.random.normal(ks[6], (C,), dtype=jnp.float32) * 0.01
        return {'fuse': fuse, 'Wq': Wq, 'bq': bq, 'Wk': Wk, 'bk': bk, 'Wv': Wv, 'bv': bv}
    _L0_conv_all = _L0_conv_setup()
    _L0_conv_in = {k: v for k, v in _L0_conv_all.items() if k in ('Wq', 'bq', 'Wk', 'bk', 'Wv', 'bv', )}
    del _L0_conv_all

    def _L0_ffn_setup():
        import math
        import jax, jax.numpy as jnp
        import numpy as np
        CAPACITY_FACTOR = 1.25
        key = jax.random.key(seed)
        ks = jax.random.split(key, 5)
        B, L, D, F, E = (8, 8192, 256, 1024, 8)
        h = jax.random.normal(ks[0], (B, L, D), dtype=jnp.float32)
        gate_w = jax.random.normal(ks[1], (D, E), dtype=jnp.float32) * 0.02
        gate_b = jnp.zeros((E,), dtype=jnp.float32)
        w1 = jax.random.normal(ks[2], (E, D, F), dtype=jnp.float32) * (1.0 / math.sqrt(D))
        b1 = jnp.zeros((E, F), dtype=jnp.float32)
        w2 = jax.random.normal(ks[3], (E, F, D), dtype=jnp.float32) * (1.0 / math.sqrt(F))
        b2 = jnp.zeros((E, D), dtype=jnp.float32)
        return {'h': h, 'gate_w': gate_w, 'gate_b': gate_b, 'w1': w1, 'b1': b1, 'w2': w2, 'b2': b2}
    _L0_ffn_all = _L0_ffn_setup()
    _L0_ffn_in = {k: v for k, v in _L0_ffn_all.items() if k in ('gate_w', 'gate_b', 'w1', 'b1', 'w2', 'b2', )}
    del _L0_ffn_all

    return {
        "x": x,
        "L0_conv_Wq": _L0_conv_in["Wq"],
        "L0_conv_bq": _L0_conv_in["bq"],
        "L0_conv_Wk": _L0_conv_in["Wk"],
        "L0_conv_bk": _L0_conv_in["bk"],
        "L0_conv_Wv": _L0_conv_in["Wv"],
        "L0_conv_bv": _L0_conv_in["bv"],
        "L0_ffn_gate_w": _L0_ffn_in["gate_w"],
        "L0_ffn_gate_b": _L0_ffn_in["gate_b"],
        "L0_ffn_w1": _L0_ffn_in["w1"],
        "L0_ffn_b1": _L0_ffn_in["b1"],
        "L0_ffn_w2": _L0_ffn_in["w2"],
        "L0_ffn_b2": _L0_ffn_in["b2"],
    }

def reference(x, L0_conv_Wq, L0_conv_bq, L0_conv_Wk, L0_conv_bk, L0_conv_Wv, L0_conv_bv, L0_ffn_gate_w, L0_ffn_gate_b, L0_ffn_w1, L0_ffn_b1, L0_ffn_w2, L0_ffn_b2):
    import jax
    import jax.numpy as jnp
    def _L0_conv_ref(fuse, Wq, bq, Wk, bk, Wv, bv):
        import jax, jax.numpy as jnp
        import numpy as np
        CUTOFF = 0.05

        def _freq_filter(x_chw, filter_type):
            x = jax.lax.stop_gradient(x_chw)
            C, H, W = x.shape
            a = jnp.abs(x)
            mn = a.min(axis=(1, 2), keepdims=True)
            ptp = a.max(axis=(1, 2), keepdims=True) - mn
            q = jnp.floor(255.0 * (a - mn) / ptp)
            f = jnp.fft.fftshift(jnp.fft.fft2(q), axes=(-2, -1))
            crow, ccol = (H // 2, W // 2)
            dr, dc = (int(CUTOFF * crow), int(CUTOFF * ccol))
            m = jnp.zeros((H, W), dtype=q.dtype)
            m = m.at[crow - dr:crow + dr, ccol - dc:ccol + dc].set(1.0)
            if filter_type == 'low_pass':
                m = 1.0 - m
            out = jnp.abs(jnp.fft.ifft2(jnp.fft.ifftshift(f * m, axes=(-2, -1))))
            return out.astype(x_chw.dtype)

        def _conv1x1(x, w, b):
            return jnp.einsum('oc,bchw->bohw', w, x) + b[None, :, None, None]
        B, C, H, W = fuse.shape
        scale = 1.0 / C ** 0.5
        FQ = jnp.broadcast_to(_freq_filter(fuse[0], 'high_pass'), fuse.shape)
        FK = jnp.broadcast_to(_freq_filter(fuse[0], 'low_pass'), fuse.shape)
        fuse_Query = _conv1x1(FQ, Wq, bq).reshape(B, C, H * W)
        fuse_Q_mask = fuse_Query.reshape(B * H, C * W)
        fuse_Query_t = jnp.transpose(fuse_Query, (0, 2, 1))
        fuse_Key = _conv1x1(FK, Wk, bk).reshape(B, C, H * W)
        Fuse_Q_mask = jnp.max(fuse_Q_mask, axis=0, keepdims=True)
        mask_KQ = jnp.einsum('bnc,bcm->bnm', fuse_Query_t, fuse_Key) * scale
        mask_KQ = jax.nn.softmax(mask_KQ, axis=0)
        mask_KQ = jnp.max(mask_KQ, axis=1)
        mask_KQ = mask_KQ.reshape(-1, W)
        mask_KQ = jnp.max(mask_KQ, axis=-1, keepdims=True)
        mask = (mask_KQ @ Fuse_Q_mask).reshape(B, C, H, W)
        fuse_Value = _conv1x1(fuse, Wv, bv)
        return fuse_Value + fuse_Value * mask

    def _L0_ffn_ref(h, gate_w, gate_b, w1, b1, w2, b2):
        import math
        import jax, jax.numpy as jnp
        import numpy as np
        CAPACITY_FACTOR = 1.25
        B, L, D = h.shape
        E = gate_w.shape[1]
        T = B * L
        C = max(1, math.ceil(CAPACITY_FACTOR * T / E))
        x = h.reshape(T, D)
        logits = x @ gate_w + gate_b
        probs = jax.nn.softmax(logits, axis=-1)
        idx = jnp.argmax(probs, axis=-1)
        prb = jnp.take_along_axis(probs, idx[:, None], axis=1)[:, 0]
        one_hot = jax.nn.one_hot(idx, E, dtype=jnp.float32)
        pos = (jnp.cumsum(one_hot, axis=0) * one_hot).sum(-1).astype(jnp.int32) - 1
        kept = pos < C
        pos_safe = jnp.where(kept, pos, C)
        buf = jnp.zeros((E, C, D), dtype=h.dtype).at[idx, pos_safe].set(x, mode='drop')
        hmid = jax.nn.relu(jnp.einsum('ecd,edf->ecf', buf, w1) + b1[:, None, :])
        ybuf = jnp.einsum('ecf,efd->ecd', hmid, w2) + b2[:, None, :]
        pos_g = jnp.minimum(pos, C - 1)
        y_tok = ybuf[idx, pos_g] * (prb * kept)[:, None]
        y = y_tok.reshape(B, L, D)
        y = jnp.nan_to_num(y, nan=0.0, posinf=10000.0, neginf=-10000.0)
        return y

    def _gn(v, G=32, eps=1e-5):
        B_, C_, H_, W_ = v.shape
        g = v.reshape(B_, G, C_ // G, H_, W_)
        m = jnp.mean(g, axis=(2, 3, 4), keepdims=True)
        s = jnp.var(g, axis=(2, 3, 4), keepdims=True)
        return ((g - m) / jnp.sqrt(s + eps)).reshape(v.shape)

    def _ln_c(v, eps=1e-6):
        m = jnp.mean(v, axis=1, keepdims=True)
        s = jnp.var(v, axis=1, keepdims=True)
        return (v - m) / jnp.sqrt(s + eps)

    def _ln_t(v, eps=1e-5):
        m = jnp.mean(v, axis=-1, keepdims=True)
        s = jnp.var(v, axis=-1, keepdims=True)
        return (v - m) / jnp.sqrt(s + eps)

    def _to_tokens(v):
        B_, C_, H_, W_ = v.shape
        return v.reshape(B_, C_, H_ * W_).transpose(0, 2, 1)
    def _from_tokens(t, like):
        B_, C_, H_, W_ = like.shape
        return t.transpose(0, 2, 1).reshape(B_, C_, H_, W_)

    x = x + _L0_conv_ref(_ln_c(x), L0_conv_Wq, L0_conv_bq, L0_conv_Wk, L0_conv_bk, L0_conv_Wv, L0_conv_bv)
    t = _to_tokens(x)
    t = t + _L0_ffn_ref(_ln_t(t), L0_ffn_gate_w, L0_ffn_gate_b, L0_ffn_w1, L0_ffn_b1, L0_ffn_w2, L0_ffn_b2)
    x = _from_tokens(t, x)
    return x


_drawn_inputs = setup_inputs


def setup_inputs(seed=0):
    import zlib

    import numpy as np

    out = dict(_drawn_inputs(seed))
    spreads = {'L0_ffn_gate_b': (0.0, 0.8), 'L0_ffn_b1': (0.0, 2.0), 'L0_ffn_b2': (0.0, 2.0)}
    factors = {'L0_conv_bq': 200.0,
     'L0_conv_bv': 5.401,
     'L0_ffn_gate_w': 8.0,
     'L0_ffn_w1': 8.0,
     'L0_ffn_w2': 8.0}
    for name, (base, spread) in spreads.items():
        noise = np.random.default_rng([zlib.crc32(name.encode()), seed]).standard_normal(out[name].shape)
        drawn = base * np.exp(spread * noise) if base else spread * noise
        out[name] = jnp.asarray(drawn.astype(out[name].dtype))
    for name, factor in factors.items():
        out[name] = (out[name] * factor).astype(out[name].dtype)
    return out
```

```python
from contextlib import ExitStack

import numpy as np

import concourse.bass as bass
from concourse import mybir

F32 = mybir.dt.float32
F32R = mybir.dt.float32r
F16 = mybir.dt.float16
BF16 = mybir.dt.bfloat16
I32 = mybir.dt.int32
ALU = mybir.AluOpType
ACT = mybir.ActivationFunctionType
AXX = mybir.AxisListType.X

C, H, W = 256, 96, 96
HW = H * W
P = 128
KC = C // P
NT = HW // P
CT = 4
CHUNK = CT * P
NCH = HW // CHUNK
E, FF = 8, 1024
KF = FF // P
CAP = 1440
SLOTS = E * CAP
STEP = 480
SP_ = 120
SJ = STEP // SP_
STEPS = SLOTS // STEP
EXPERT_STEPS = CAP // STEP
ROW = C + 2
ROWS = 12288
NOWHERE = 1 << 20
PERIOD = 24576 // P
NB = 23
NSYM = 9
PART = 32
ROUND = 12582912.0
SLACK = 0.5 - 2.0 ** -14
FMAX = 3.4028234663852886e38


def hold(eng, semaphore, n, held):
    eng.wait_ge(semaphore, n)
    if not isinstance(n, int):
        eng.sem_inc(held, 1)


def past(k, n):
    return not isinstance(k, int) or k >= n


def pipeline(eng, n, turn, stages):
    longest = max(lag for lag, _ in stages)
    head = -(-(longest + 2) // turn)

    def fixed(s):
        for lag, stage in stages:
            k = s - lag
            if 0 <= k < n:
                stage(k, k % turn, lambda d, k=k: k // d)

    for s in range(head * turn):
        fixed(s)
    with eng.Fori(head, n // turn) as i:
        for q in range(turn):
            for lag, stage in stages:
                stage(i * turn + (q - lag), (q - lag) % turn,
                      lambda d, q=q, lag=lag: i * (turn // d) + (q - lag) // d)
    for s in range(n, n + longest):
        fixed(s)


def program(nc, x, wqT, bq, wvT, bv, gate_w, gate_b, w1, b1T, w2, b2T, fwd, inv, out):
    ctx = ExitStack()
    with ctx:
        def sem(name):
            return ctx.enter_context(nc.semaphore(name))

        def sb(name, shape, dt, where=ctx):
            return where.enter_context(nc.sbuf_tensor(name, shape, dt))

        slot_rows = nc.dram_tensor("slot_rows", (ROWS, ROW), F32, kind="Internal").ap()
        token_y = nc.dram_tensor("token_y", (HW, C), F32, kind="Internal").ap()

        xt = sb("xt", [P, NT, C], F32)
        ident = sb("ident", [P, P], F32)
        gate_col = sb("gate_col", [P, KC, E], F32)
        b1s = sb("b1s", [P, E * KF], F32)
        b2s = sb("b2s", [P, E * KC], F32)

        one = ExitStack()
        fc = sb("fc", [P, KC, HW], F32, one)
        query_scope = ExitStack()
        wq_hl = sb("wq_hl", [P, 2, KC, C], F32R, query_scope)
        query_scope.close()
        gate1 = sb("gate1", [P, 2 * KC * C], F32, one)
        wv_hl = sb("wv_hl", [P, 2, KC, C], F32R, one)
        biases = sb("biases", [2, 2, C], F32R, one)
        bias_scope = ExitStack()
        bias_raw = sb("bias_raw", [2, 2, C], F32, bias_scope)
        bias_hi = sb("bias_hi", [2, 2, C], F32R, bias_scope)
        bias_scope.close()
        m8 = sb("m8", [P, E * NT], F32, one)
        lg = sb("lg", [P, CT, E], F32, one)
        ex = sb("ex", [P, CT, E], F32, one)
        pick = sb("pick", [P, CT, E], F32, one)
        place = sb("place", [P, E, CT], F32, one)
        waves = sb("waves", [3 * PART, 2, KC, P], F16, one)
        run = sb("run", [P, E, CT + 1], BF16, one)
        top, idx, pos, raw_slot, over_cap, den = (sb(n, [P, CT], F32, one) for n in
                                                  ("top", "idx", "pos", "raw_slot", "over_cap", "den"))
        slot = [sb(f"slot{b}", [P, CT], I32, one) for b in range(3)]
        mv = sb("mv", [P, CT, 2], F32, one)
        ones2 = sb("ones2", [2, P], F32R, one)
        sums_scope = ExitStack()
        basis_f = sb("basis_f", [P, NT, 3 * NB], BF16, sums_scope)
        qT = [sb(f"qT{b}", [P, CT, C], BF16, sums_scope) for b in range(2)]
        dft = sb("dft", [P, KC, 3 * NB], F32, sums_scope)
        coef = sb("coef", [P, KC, 2, NB], F32, sums_scope)
        coef16 = sb("coef16", [P, KC, 2, 3 * PART], F16, sums_scope)
        most = sb("most", [P, KC, NCH], F32, sums_scope)
        least = sb("least", [P, KC, NCH], F32, sums_scope)
        sums_scope.close()
        hi = [sb(f"hi{b}", [P, KC, CHUNK], F32R, one) for b in range(2)]
        lo = [sb(f"lo{b}", [P, KC, CHUNK], F32R, one) for b in range(2)]
        work = [sb(f"work{b}", [P, 1024], F32, one) for b in range(4)]
        ut = sb("ut", [P, 3 * CT, ROW], F32, one)
        ident16 = sb("ident16", [P, P], F16, one)
        bn6 = sb("bn6", [P, CT, 6], F32, one)
        rstd = sb("rstd", [P, CT], F32, one)
        eps = sb("eps", [P, 2], F32, one)
        std = sb("std", [P, CT], F32, one)
        qs = sb("qs", [P, 6, KC], F32, one)
        gb_row = sb("gb_row", [1, E], F32, one)
        ones1 = sb("ones1", [2, P], F32, one)
        tri = sb("tri", [P, P], BF16, one)
        ones_b = sb("ones_b", [P, P], BF16, one)
        iota_e = sb("iota_e", [P, CT, E], F32, one)
        tok_no = sb("tok_no", [P, NT], I32, one)
        reset = sb("reset", [P, E * (CT + 1)], F32, one)
        hot = sb("hot", [P, E, CT + 1], BF16, one)
        one.close()

        two = ExitStack()
        w_raw = sb("w_raw", [P, KC * FF], F32, two)
        w1_hl = [sb(f"w1_hl{b}", [P, 2, KC, FF], F32R, two) for b in range(2)]
        w2_hl = [sb(f"w2_hl{b}", [P, 2, KF, C], F32R, two) for b in range(2)]
        rows = [sb(f"rows{b}", [SP_, SJ, ROW], F32, two) for b in range(3)]
        x_hl = [sb(f"x_hl{b}", [P, 2, KC, STEP], F32R, two) for b in range(2)]
        h32 = [sb(f"h32_{b}", [P, STEP], F32, two) for b in range(2)]
        h_hl = [sb(f"h_hl{b}", [P, 2, STEP], F32R, two) for b in range(3)]
        y32 = sb("y32", [P, KC, STEP], F32, two)
        y_bad = sb("y_bad", [SP_, 2 * C], I32, two)
        y_fix = sb("y_fix", [SP_, 2 * C], F32, two)
        y_nil = sb("y_nil", [SP_, 2 * C], F32, two)
        y_neg = sb("y_neg", [SP_, 2 * C], F32, two)
        y_rows = [sb(f"y_rows{b}", [SP_, SJ, C], F32, two) for b in range(2)]
        two.close()

        three = ExitStack()
        y_in = [sb(f"y_in{b}", [P, CT, C], F32, three) for b in range(2)]
        total = [sb(f"total{b}", [P, CT, C], F32, three) for b in range(2)]
        planar = [sb(f"planar{b}", [P, KC, CHUNK], F32, three) for b in range(2)]
        three.close()

        banks = ctx.enter_context(nc.psum_tensor("banks", [P, 8, 512], F32))

        def tokens_of(bank):
            return banks[:, bank:bank + 2, :].rearrange("p u (v c) -> p (u v) c", c=C)

        consts_loaded = sem("consts_loaded")
        made = sem("made")
        pool_ready = sem("pool_ready")
        split_ready = sem("split_ready")
        blank_ready = sem("blank_ready")
        blanks = sem("blanks")
        x_turned = sem("x_turned")
        x_kept = sem("x_kept")
        bn_done = sem("bn_done")
        mv_done = sem("mv_done")
        rstd_done = sem("rstd_done")
        std_done = sem("std_done")
        std2_done = sem("std2_done")
        held = sem("held")
        f_ready = sem("f_ready")
        f_turned = sem("f_turned")
        f_kept = sem("f_kept")
        ranged = sem("ranged")
        range_steps = sem("range_steps")
        magnitudes = sem("magnitudes")
        scaled = sem("scaled")
        q_turned = sem("q_turned")
        qT_ready = sem("qT_ready")
        dft_done = sem("dft_done")
        coef_steps = sem("coef_steps")
        coef_turned = sem("coef_turned")
        waves_ready = sem("waves_ready")
        waved = sem("waved")
        squared = sem("squared")
        power_ready = sem("power_ready")
        root_ready = sem("root_ready")
        fq_hi = sem("fq_hi")
        fq_lo = sem("fq_lo")
        queried = sem("queried")
        m8_ready = sem("m8_ready")
        gate_steps = sem("gate_steps")
        v_hi = sem("v_hi")
        v_lo = sem("v_lo")
        v_done = sem("v_done")
        gated = sem("gated")
        x1_ready = sem("x1_ready")
        bn2_done = sem("bn2_done")
        mv2_done = sem("mv2_done")
        rstd2_done = sem("rstd2_done")
        u_ready = sem("u_ready")
        u_turned = sem("u_turned")
        u_kept = sem("u_kept")
        logits = sem("logits")
        route = sem("route")
        exp_done = sem("exp_done")
        counted = sem("counted")
        w1_loaded = sem("w1_loaded")
        w2_loaded = sem("w2_loaded")
        w_hi = sem("w_hi")
        w_lo = sem("w_lo")
        rows_turned = sem("rows_turned")
        xe_hi = sem("xe_hi")
        xe_lo = sem("xe_lo")
        up_done = sem("up_done")
        h_ready = sem("h_ready")
        h_hi = sem("h_hi")
        h_lo = sem("h_lo")
        down_done = sem("down_done")
        step_done = sem("step_done")
        y0_kept = sem("y0_kept")
        y1_kept = sem("y1_kept")
        y_turned = sem("y_turned")
        y_scaled = sem("y_scaled")
        y_guard = sem("y_guard")
        summed = sem("summed")
        sum_turned = sem("sum_turned")
        sum_kept = sem("sum_kept")
        const_v = sem("const_v")
        x_loaded = [sem(f"x_loaded{b}") for b in range(2)]
        basis_loaded = [sem(f"basis_loaded{b}") for b in range(2)]
        scattered = [sem(f"scattered{b}") for b in range(3)]
        rows_loaded = [sem(f"rows_loaded{b}") for b in range(3)]
        y_out = [sem(f"y_out{b}") for b in range(2)]
        y_loaded = [sem(f"y_loaded{b}") for b in range(2)]
        stored = [sem(f"stored{b}") for b in range(2)]

        PAIR = 2 * EXPERT_STEPS
        PAIRS = E // 2
        work_uc = [t[:, :].rearrange("p (u n) -> p u n", u=KC) for t in work]
        work_jc = [t[:, :].rearrange("p (j c) -> p j c", j=CT) for t in work]
        im_sq = [ut[:, 4 * b:4 * b + 4, :].rearrange("p a c -> p (a c)")[:, 0:1024] for b in range(2)]
        basis_i = [ut[0:3 * PART, 8 + b, 0:CHUNK // 2].bitcast(F16) for b in range(2)]
        blank = ut[:, 11:12, :]
        MADE, CONSTS, CONST_V, ROUTE = 11, 11, 8, 16
        BLANKS = ROWS // P // 12 + NT // 12
        block = ctx.enter_context(nc.Block())

        @block.sync
        def _(sp):
            for dst, src in ((basis_f[:, :, :], fwd), (gate_col[:, :, :], gate_w.rearrange("(u p) e -> p u e", p=P)),
                             (b1s[:, :], b1T), (b2s[:, :], b2T), (gb_row[:, :], gate_b),
                             (work_uc[2][:, :, 0:C], wqT.rearrange("(u p) o -> p u o", p=P)),
                             (work_uc[3][:, :, 0:C], wvT.rearrange("(u p) o -> p u o", p=P)),
                             (bias_raw[0:1, 0, :], bq), (bias_raw[1:2, 0, :], bq),
                             (bias_raw[0:1, 1, :], bv), (bias_raw[1:2, 1, :], bv)):
                sp.dma_start(dst, src).then_inc(consts_loaded, 16)

            def load_x(k, m, over):
                if past(k, 2):
                    hold(sp, x_turned, k - 1, held)
                sp.dma_start(work_uc[m][:, :, :], x.rearrange("(u p) n -> p u n", p=P)[:, :, bass.ds(k * CHUNK, CHUNK)]
                             ).then_inc(x_loaded[m], 16)

            pipeline(sp, NCH, 2, [(0, load_x)])

            def load_basis(k, m, over):
                if past(k, 2):
                    hold(sp, waved, k - 1, held)
                sp.dma_start(basis_i[m], inv[:, bass.ds(k * CHUNK, CHUNK)]).then_inc(basis_loaded[m], 16)

            pipeline(sp, NCH, 2, [(0, load_basis)])

            sp.wait_ge(route, ROUTE * NCH)
            sp.wait_ge(logits, NCH)
            for m in range(3):
                sp.wait_ge(scattered[m], 16 * CT * NCH // 3)

            def load_rows(s, m, third):
                if past(s, 3):
                    hold(sp, y_out[(m - 3) % 2], third[1], held)
                sp.dma_start(rows[m % 3][:, :, :],
                             slot_rows[bass.ds(s * STEP, STEP), :].rearrange("(j p) c -> p j c", p=SP_)
                             ).then_inc(rows_loaded[m % 3], 16)

            def load_w1(e):
                if past(e, 1):
                    hold(sp, w_lo, e * 2, held)
                sp.dma_start(w_raw[:, :].rearrange("p (u f) -> p u f", u=KC),
                             w1[bass.ds(e, 1), :, :].rearrange("e (u p) f -> p (e u) f", p=P)).then_inc(w1_loaded, 16)

            def load_w2(e):
                hold(sp, w_lo, e * 2 + 1, held)
                sp.dma_start(w_raw[:, :].rearrange("p (u c) -> p u c", u=KF),
                             w2[bass.ds(e, 1), :, :].rearrange("e (u p) c -> p (e u) c", p=P)).then_inc(w2_loaded, 16)

            load_w1(0)
            load_rows(0, 0, None)
            load_rows(1, 1, None)
            load_w2(0)

            def pair(i, first, last):
                for m in range(PAIR):
                    if m % EXPERT_STEPS == 0 and not (last and m):
                        load_w1(i * 2 + m // EXPERT_STEPS + 1)
                        load_w2(i * 2 + m // EXPERT_STEPS + 1)
                    if not (last and m + 2 >= PAIR):
                        load_rows(i * PAIR + m + 2, m + 2, (0, i * (CT * 16 * 3) + CT * 16 * ((m - 1) // 2 + 1)))

            pair(0, True, False)
            with sp.Fori(1, PAIRS - 1) as i:
                pair(i, False, False)
            pair(PAIRS - 1, False, True)

            for b in range(2):
                sp.wait_ge(y_out[b], 16 * SJ * STEPS // 2)

            def load_y(k, m, over):
                if past(k, 2):
                    hold(sp, summed, k - 1, held)
                sp.dma_start(y_in[m][:, :, :],
                             token_y[bass.ds(k * CHUNK, CHUNK), :].rearrange("(j p) c -> p j c", p=P)
                             ).then_inc(y_loaded[m], 16)

            def store(k, m, over):
                hold(sp, sum_kept, k + 1, held)
                sp.dma_start(out.rearrange("(u p) n -> p u n", p=P)[:, :, bass.ds(k * CHUNK, CHUNK)],
                             planar[m][:, :, :]).then_inc(stored[m], 16)

            pipeline(sp, NCH, 2, [(0, load_y), (1, store)])
            for b in range(2):
                sp.wait_ge(stored[b], 16 * NCH // 2)

        @block.gpsimd
        def _(pool):
            pool.memset(ident[:, :], 0.0).then_inc(made, 1)
            pool.memset(ident16[:, :], 0.0).then_inc(made, 1)
            pool.memset(tri[:, :], 1.0).then_inc(made, 1)
            pool.memset(blank[:, :, :], 0.0).then_inc(made, 1)
            pool.memset(reset[:, :], 1.0).then_inc(made, 1)
            pool.memset(ones_b[:, :], 1.0)
            pool.memset(ones1[:, :], 1.0)
            pool.memset(eps[:, 0:1], 1e-6)
            pool.memset(eps[:, 1:2], 1e-5)
            pool.memset(hot[:, :, :], 0.0)
            pool.memset(coef16[:, :, :, :], 0.0)
            pool.iota(iota_e[:, :, :], pattern=[[0, CT], [1, E]], base=0, channel_multiplier=0,
                      allow_small_or_imprecise_dtypes=True)
            pool.iota(tok_no[:, :], pattern=[[P, NT]], base=0, channel_multiplier=1).then_inc(made, 1)
            pool.wait_ge(made, 6)
            for m in (ident, ident16):
                pool.affine_select(out=m[:, :], in_=m[:, :], compare_op=ALU.not_equal, fill=1.0, base=0,
                                   pattern=[[-1, P]], channel_multiplier=1).then_inc(made, 1)
            pool.affine_select(out=tri[:, :], in_=tri[:, :], compare_op=ALU.is_ge, fill=0.0, base=0,
                               pattern=[[1, P]], channel_multiplier=-1).then_inc(made, 1)
            pool.memset(blank[:, :, C + 1:ROW].bitcast(I32), NOWHERE).then_inc(made, 1)
            pool.memset(reset[:, :].rearrange("p (e t) -> p e t", e=E)[:, :, 0:1], 0.0).then_inc(made, 1)

            pool.wait_ge(made, MADE)
            pool.wait_ge(x_turned, NCH - 2)
            for q in range(ROWS // P // 12):
                pool.dma_start(slot_rows.rearrange("(p r) c -> p r c", p=P)[:, q * 12:q * 12 + 12, :], blank[:, :, :].broadcast_to([P, 12, ROW])
                               ).then_inc(blanks, 16)
            for q in range(NT // 12):
                pool.dma_start(token_y.rearrange("(p r) c -> p r c", p=P)[:, q * 12:q * 12 + 12, :], blank[:, :, 0:C].broadcast_to([P, 12, C])
                               ).then_inc(blanks, 16)

            def power(k, m, over):
                hold(pool, squared, k * 2 + 2, held)
                if past(k, 2):
                    hold(pool, fq_lo, k - 1, held)
                pool.tensor_tensor(work[2 + m][:, :], work[m][:, :], im_sq[m][:, :], ALU.add).then_inc(power_ready, 1)

            pipeline(pool, NCH, 2, [(0, power)])

            pool.wait_ge(blanks, 16 * BLANKS)

            def rest(k, m, over):
                hold(pool, v_hi, k + 1, held)
                pool.tensor_tensor(lo[m % 2][:, :, :], fc[:, :, bass.ds(k * CHUNK, CHUNK)],
                                   hi[m % 2][:, :, :], ALU.subtract).then_inc(v_lo, 1)

            def residual(k, m, over):
                hold(pool, gated, k + 1, held)
                chunk = xt[:, bass.ds(k * CT, CT), :]
                pool.tensor_tensor(chunk, chunk, work_jc[m % 2][:, :, :], ALU.add).then_inc(x1_ready, 1)

            def scatter(k, m, over):
                hold(pool, route, k * ROUTE + ROUTE, held)
                for j in range(CT):
                    pool.indirect_dma_start(
                        out=slot_rows[:, :], out_offset=bass.IndirectOffsetOnAxis(slot[m % 3][:, j:j + 1], 0),
                        in_=ut[:, m % 3 * CT + j, :], in_offset=None, bounds_check=SLOTS - 1, oob_is_err=False,
                    ).then_inc(scattered[m % 3], 16)

            pipeline(pool, NCH, 6, [(0, rest), (1, residual), (3, scatter)])

            def split(e, b):
                if past(e, 2):
                    hold(pool, step_done, (e - 1) * EXPERT_STEPS, held)
                hold(pool, w1_loaded, e * 16 + 16, held)
                raw1 = w_raw[:, :].rearrange("p (u f) -> p u f", u=KC)
                pool.tensor_copy(w1_hl[b][:, 0, :, :], raw1).then_inc(w_hi, 1)
                hold(pool, w_hi, e * 2 + 1, held)
                pool.tensor_tensor(w1_hl[b][:, 1, :, :], raw1, w1_hl[b][:, 0, :, :], ALU.subtract).then_inc(w_lo, 1)
                hold(pool, w2_loaded, e * 16 + 16, held)
                raw2 = w_raw[:, :].rearrange("p (u c) -> p u c", u=KF)
                pool.tensor_copy(w2_hl[b][:, 0, :, :], raw2).then_inc(w_hi, 1)
                hold(pool, w_hi, e * 2 + 2, held)
                pool.tensor_tensor(w2_hl[b][:, 1, :, :], raw2, w2_hl[b][:, 0, :, :], ALU.subtract).then_inc(w_lo, 1)

            def scatter_y(s, m):
                for r in range(2):
                    hold(pool, y_guard, s * 12 + 6 * r + 6, held)
                    for j in (2 * r, 2 * r + 1):
                        pool.indirect_dma_start(
                            out=token_y[:, :],
                            out_offset=bass.IndirectOffsetOnAxis(rows[m % 3][:, j, C + 1:ROW].bitcast(I32), 0),
                            in_=y_rows[m % 2][:, j, :], in_offset=None, bounds_check=HW - 1, oob_is_err=False,
                        ).then_inc(y_out[m % 2], 16)

            split(0, 0)

            def pair(i, first, last):
                for m in range(PAIR):
                    if m % EXPERT_STEPS == 0 and not (last and m):
                        split(i * 2 + m // EXPERT_STEPS + 1, (m // EXPERT_STEPS + 1) % 2)
                    if not (first and m == 0):
                        scatter_y(i * PAIR + (m - 1), m - 1)
                if last:
                    scatter_y(STEPS - 1, PAIR - 1)

            pair(0, True, False)
            with pool.Fori(1, PAIRS - 1) as i:
                pair(i, False, False)
            pair(PAIRS - 1, False, True)

        @block.scalar
        def _(act):
            def keep_x(k, m, over):
                hold(act, x_turned, k + 1, held)
                act.activation(xt[:, bass.ds(k * CT, CT), :], tokens_of(2 * m), ACT.Copy).then_inc(x_kept, 1)

            def keep_f(k, m, over):
                hold(act, f_turned, k + 1, held)
                act.activation(fc[:, :, bass.ds(k * CHUNK, CHUNK)], banks[:, 4 + 2 * m:6 + 2 * m, :], ACT.Copy
                               ).then_inc(f_kept, 1)

            def deviation(k, n, variances, done):
                hold(act, variances, k * CT + CT, held)
                act.activation(std[:, :], mv[:, :, 1], ACT.Sqrt, bias=eps[:, n:n + 1]).then_inc(done, 1)

            pipeline(act, NCH, 2, [(0, keep_x), (1, keep_f),
                                   (0, lambda k, m, over: deviation(k, 0, mv_done, std_done))])

            act.wait_ge(ranged, NCH)

            def magnitude(k, m, over):
                if past(k, 2):
                    hold(act, scaled, k - 1, held)
                act.activation(work_uc[m][:, :, :], fc[:, :, bass.ds(k * CHUNK, CHUNK)], ACT.Abs).then_inc(magnitudes, 1)

            pipeline(act, NCH, 2, [(0, magnitude)])

            def square(k, m, over):
                hold(act, waved, k + 1, held)
                act.activation(work_uc[m][:, :, :], banks[:, 0:2, :], ACT.Square).then_inc(squared, 1)
                act.activation(im_sq[m][:, :].rearrange("p (u n) -> p u n", u=KC), banks[:, 2:4, :], ACT.Square
                               ).then_inc(squared, 1)

            def root(k, m, over):
                hold(act, power_ready, k + 1, held)
                act.activation(work[2 + m][:, :], work[2 + m][:, :], ACT.Sqrt).then_inc(root_ready, 1)

            pipeline(act, NCH, 2, [(0, square), (1, root)])

            act.wait_ge(queried, NCH)
            def value_hi(k, m, over):
                if past(k, 2):
                    hold(act, v_done, k - 1, held)
                act.activation(hi[m % 2][:, :, :], fc[:, :, bass.ds(k * CHUNK, CHUNK)], ACT.Copy).then_inc(v_hi, 1)

            def exps(k, m, over):
                hold(act, route, k * ROUTE + 2, held)
                act.activation(ex[:, :, :], lg[:, :, :], ACT.Exp).then_inc(exp_done, 1)

            def keep_u(k, m, over):
                hold(act, u_turned, k + 1, held)
                act.activation(work_uc[2 + m % 2][:, :, :], banks[:, 2:4, :], ACT.Copy).then_inc(u_kept, 1)

            pipeline(act, NCH, 6, [(0, value_hi), (2, lambda k, m, over: deviation(k, 1, mv2_done, std2_done)),
                                   (3, exps), (2, keep_u)])

            def x_rounded(s, m):
                hold(act, rows_turned, s + 1, held)
                act.activation(x_hl[m % 2][:, 0, :, :], banks[:, 5:7, 0:STEP], ACT.Copy).then_inc(xe_hi, 1)

            def hidden(s, m, f, i):
                g = s * KF + f
                hold(act, up_done, g + 1, held)
                if past(s, 1) or f >= 2:
                    hold(act, h_lo, g - 1, held)
                if past(s, 1) or f >= 3:
                    hold(act, down_done, g - 2, held)
                bias = b1s[:, bass.ds((i * 2 + m // EXPERT_STEPS) * KF + f, 1)]
                part = banks[:, (m * KF + f) % 3, 0:STEP]
                act.activation(h_hl[(m * KF + f) % 3][:, 0, :], part, ACT.Relu, bias=bias)
                act.activation(h32[f % 2][:, :], part, ACT.Relu, bias=bias).then_inc(h_ready, 1)

            def keep_y0(s, m, i):
                hold(act, step_done, s + 1, held)
                if past(s, 1):
                    hold(act, y_turned, s * 2, held)
                act.activation(y32[:, 0, :], banks[:, 3, 0:STEP], ACT.Identity,
                               bias=b2s[:, bass.ds((i * PAIR + m) // EXPERT_STEPS * KC if isinstance(i, int)
                                                   else (i * 2 + m // EXPERT_STEPS) * KC, 1)]).then_inc(y0_kept, 1)

            def scale_y(s, m, r, left):
                if past(s, 2) and r == 0:
                    hold(act, y_out[m % 2], left, held)
                hold(act, y_turned, s * 2 + r + 1, held)
                for jj in range(2):
                    j = 2 * r + jj
                    last = act.activation(y_rows[m % 2][:, j, :], banks[0:SP_, 7, jj * C:(jj + 1) * C], ACT.Copy,
                                          scale=rows[m % 3][:, j, C:C + 1])
                last.then_inc(y_scaled, 1)

            x_rounded(0, 0)

            def pair(i, first, last):
                for m in range(PAIR):
                    s = i * PAIR + m
                    for f in range(KF):
                        hidden(s, m, f, i)
                        if f == 2 and not (first and m == 0):
                            keep_y0(i * PAIR + (m - 1), m - 1, i)
                        if f == 5 and not (last and m == PAIR - 1):
                            x_rounded(i * PAIR + (m + 1), m + 1)
                        if f in (3, 5) and not (first and m == 0):
                            scale_y(i * PAIR + (m - 1), m - 1, (f - 3) // 2,
                                    i * (3 * SJ * 16) + SJ * 16 * ((m - 1) // 2))
                if last:
                    keep_y0(STEPS - 1, PAIR - 1, i)
                    for r in range(2):
                        scale_y(STEPS - 1, PAIR - 1, r, 16 * SJ * ((STEPS - 1) // 2))

            pair(0, True, False)
            with act.Fori(1, PAIRS - 1) as i:
                pair(i, False, False)
            pair(PAIRS - 1, False, True)

            def keep_sum(k, m, over):
                hold(act, sum_turned, k + 1, held)
                if past(k, 2):
                    hold(act, stored[m], over(2) * 16, held)
                act.activation(planar[m][:, :, :], banks[:, 2 * m:2 * m + 2, :], ACT.Copy).then_inc(sum_kept, 1)

            pipeline(act, NCH, 2, [(0, keep_sum)])

        @block.vector
        def _(dve):
            dve.wait_ge(consts_loaded, 16 * CONSTS)
            dve.wait_ge(made, MADE)
            for n, (hl, raw) in enumerate(((wq_hl, work_uc[2]), (wv_hl, work_uc[3]))):
                dve.tensor_copy(hl[:, 0, :, :], raw[:, :, 0:C]).then_inc(const_v, 1)
                dve.wait_ge(const_v, 2 * n + 1)
                dve.tensor_tensor(hl[:, 1, :, :], raw[:, :, 0:C], hl[:, 0, :, :], ALU.subtract).then_inc(const_v, 1)
            dve.tensor_copy(bias_hi[:, :, :], bias_raw[:, :, :]).then_inc(const_v, 1)
            dve.wait_ge(const_v, 5)
            dve.tensor_tensor(biases[:, :, :], bias_raw[:, :, :], bias_hi[:, :, :], ALU.subtract).then_inc(const_v, 1)
            dve.wait_ge(const_v, 6)
            dve.tensor_copy(biases[0:1, :, :], bias_hi[0:1, :, :]).then_inc(const_v, 1)
            dve.tensor_copy(ones2[:, :], ones1[:, :]).then_inc(const_v, 1)
            dve.wait_ge(const_v, CONST_V)

            def statistics(k, bn_sem, mv_sem):
                for j in range(CT):
                    dve.bn_stats(bn6[:, j, :], xt[:, bass.ds(k * CT + j, 1), :].rearrange("p j c -> p (j c)")
                                 ).then_inc(bn_sem, 1)
                hold(dve, bn_sem, k * CT + CT, held)
                for j in range(CT):
                    dve.bn_aggr(mv[:, j, :], bn6[:, j, :]).then_inc(mv_sem, 1)

            def inverse_std(k, std_sem, rstd_sem):
                dve.wait_ge(std_sem, k + 1)
                dve.reciprocal(rstd[:, :], std[:, :]).then_inc(rstd_sem, 1)
                dve.wait_ge(rstd_sem, k + 1)

            def x_statistics(k, m, over):
                dve.wait_ge(x_kept, k + 1)
                statistics(k, bn_done, mv_done)

            def normalise(k, m, over):
                inverse_std(k, std_done, rstd_done)
                if past(k, 2):
                    dve.wait_ge(f_turned, k - 1)
                for j in range(CT):
                    dve.tensor_scalar(work_jc[2 + m][:, j, :],
                                      xt[:, bass.ds(k * CT + j, 1), :].rearrange("p j c -> p (j c)"),
                                      mv[:, j, 0:1], rstd[:, j:j + 1], ALU.subtract, ALU.mult).then_inc(f_ready, 1)

            def extremes(k, m, over):
                dve.wait_ge(f_kept, k + 1)
                chunk = fc[:, :, bass.ds(k * CHUNK, CHUNK)]
                dve.tensor_reduce(most[:, :, bass.ds(k, 1)], chunk, mybir.AxisListType.X, ALU.max,
                                  apply_absolute_value=True)
                dve.tensor_reduce(least[:, :, bass.ds(k, 1)], chunk, mybir.AxisListType.X, ALU.min,
                                  apply_absolute_value=True).then_inc(ranged, 1)

            pipeline(dve, NCH, 2, [(0, x_statistics), (1, extremes), (0, normalise)])

            dve.wait_ge(ranged, NCH)
            dve.tensor_reduce(qs[:, 0, :], most[:, :, :], mybir.AxisListType.X, ALU.max).then_inc(range_steps, 1)
            dve.tensor_reduce(qs[:, 1, :], least[:, :, :], mybir.AxisListType.X, ALU.min).then_inc(range_steps, 1)
            dve.wait_ge(range_steps, 2)
            dve.tensor_tensor(qs[:, 2, :], qs[:, 0, :], qs[:, 1, :], ALU.subtract).then_inc(range_steps, 1)
            dve.wait_ge(range_steps, 3)
            dve.reciprocal(qs[:, 3, :], qs[:, 2, :]).then_inc(range_steps, 1)
            dve.scalar_tensor_tensor(qs[:, 5, :], qs[:, 2, :], SLACK / 255.0, qs[:, 1, :], ALU.mult, ALU.add
                                     ).then_inc(range_steps, 1)
            dve.wait_ge(range_steps, 5)
            dve.tensor_scalar(qs[:, 4, :], qs[:, 3, :], 255.0, None, ALU.mult).then_inc(range_steps, 1)
            dve.wait_ge(range_steps, 6)

            def scale_f(k, m, over):
                dve.wait_ge(magnitudes, k + 1)
                if past(k, 2):
                    dve.wait_ge(q_turned, k - 1)
                for u in range(KC):
                    last = dve.tensor_scalar(work_uc[2 + m][:, u, :], work_uc[m][:, u, :], qs[:, 5, u:u + 1],
                                             qs[:, 4, u:u + 1], ALU.subtract, ALU.mult)
                last.then_inc(scaled, 1)

            def levels(k, m, over):
                dve.wait_ge(q_turned, k + 1)
                if past(k, 2):
                    dve.wait_ge(dft_done, k - 1)
                dve.tensor_scalar(qT[m][:, :, :], tokens_of(2 * m), ROUND, ROUND, ALU.add, ALU.subtract).then_inc(qT_ready, 1)

            pipeline(dve, NCH, 2, [(0, scale_f), (1, levels)])

            dve.wait_ge(dft_done, NCH)
            D = dft[:, :, :]
            s = 1.0 / HW
            n_uns = (NB - NSYM) // 2
            uc, us = NSYM, NSYM + n_uns
            dve.tensor_copy(D, banks[:, 4:6, 0:3 * NB]).then_inc(coef_steps, 1)
            dve.wait_ge(coef_steps, 1)
            dve.tensor_tensor(D[:, :, NB:2 * NB], D[:, :, NB:2 * NB], D[:, :, 2 * NB:], ALU.add).then_inc(coef_steps, 1)
            dve.wait_ge(coef_steps, 2)
            dve.tensor_tensor(D[:, :, 0:NB], D[:, :, 0:NB], D[:, :, NB:2 * NB], ALU.add).then_inc(coef_steps, 1)
            dve.wait_ge(coef_steps, 3)
            dve.memset(coef[:, :, 1, 0:NSYM], 0.0).then_inc(coef_steps, 1)
            for dst, src, scale in ((coef[:, :, 0, 0:1], D[:, :, 0:1], s), (coef[:, :, 0, 1:NSYM], D[:, :, 1:NSYM], 2 * s),
                                    (coef[:, :, 0, uc:NB], D[:, :, uc:NB], s), (coef[:, :, 1, uc:us], D[:, :, us:NB], -s),
                                    (coef[:, :, 1, us:NB], D[:, :, uc:us], s)):
                dve.tensor_scalar(dst, src, scale, None, ALU.mult).then_inc(coef_steps, 1)
            dve.wait_ge(coef_steps, 9)
            dve.wait_ge(made, MADE)
            dve.tensor_copy(coef16[:, :, :, 0:NB], coef[:, :, :, :]).then_inc(coef_steps, 1)
            dve.tensor_copy(coef16[:, :, :, 2 * PART:2 * PART + NB], coef[:, :, :, :]).then_inc(coef_steps, 1)
            dve.wait_ge(coef_steps, 11)
            dve.tensor_tensor(coef16[:, :, :, PART:PART + NB], coef[:, :, :, :], coef16[:, :, :, 0:NB], ALU.subtract
                              ).then_inc(coef_steps, 1)
            dve.wait_ge(coef_turned, 1)
            dve.tensor_copy(waves[:, :, :, :].rearrange("k r u c -> k (r u c)"),
                            banks[0:3 * PART, 6, 0:256].bitcast(F16)).then_inc(waves_ready, 1)

            def split_root(k, m, over):
                dve.wait_ge(root_ready, k + 1)
                if past(k, 2):
                    dve.wait_ge(queried, k - 1)
                dve.tensor_copy(hi[m][:, :, :], work_uc[2 + m][:, :, :]).then_inc(fq_hi, 1)
                dve.wait_ge(fq_hi, k + 1)
                dve.tensor_tensor(lo[m][:, :, :], work_uc[2 + m][:, :, :], hi[m][:, :, :], ALU.subtract
                                  ).then_inc(fq_lo, 1)

            def query_max(k, m, over):
                dve.wait_ge(queried, k + 1)
                dve.tensor_reduce(m8[:, :].rearrange("p (b t) -> p t b", b=8)[:, bass.ds(k * CT, CT), :],
                                  tokens_of(4 + 2 * m).rearrange("p j (a b) -> p j b a", b=8),
                                  mybir.AxisListType.X, ALU.max).then_inc(m8_ready, 1)

            pipeline(dve, NCH, 2, [(0, split_root), (1, query_max)])

            dve.wait_ge(m8_ready, NCH)
            dve.wait_ge(blanks, 16 * BLANKS)
            dve.tensor_tensor(gate1[:, 0:PERIOD], m8[:, 0:PERIOD], m8[:, PERIOD:2 * PERIOD], ALU.max
                              ).then_inc(gate_steps, 1)
            dve.wait_ge(gate_steps, 1)
            dve.tensor_tensor(m8[:, 0:PERIOD], gate1[:, 0:PERIOD], m8[:, 2 * PERIOD:], ALU.max).then_inc(gate_steps, 1)
            dve.wait_ge(gate_steps, 2)
            for n in range(3):
                dve.tensor_scalar(gate1[:, n * PERIOD:(n + 1) * PERIOD], m8[:, 0:PERIOD], 1.0, None, ALU.add
                                  ).then_inc(gate_steps, 1)
            dve.wait_ge(gate_steps, 5)

            def gate_value(k, m, over):
                dve.wait_ge(v_done, k + 1)
                if past(k, 2):
                    dve.wait_ge(x1_ready, k - 1)
                mask = gate1[:, 0:E * NT].rearrange("p (b t) -> p t b", b=8)[:, bass.ds(k * CT, CT), :]
                dve.tensor_tensor(work[m % 2][:, :].rearrange("p (j a b) -> p j a b", j=CT, b=8),
                                  tokens_of(0).rearrange("p j (a b) -> p j a b", b=8),
                                  mask.unsqueeze(2).broadcast_to([P, CT, C // 8, 8]), ALU.mult).then_inc(gated, 1)

            def route_a(k, m, over):
                base = k * ROUTE
                dve.wait_ge(logits, k + 1)
                psg = banks[:, 4 + m % 2, 0:CT * E].rearrange("p (t e) -> p t e", e=E)
                dve.tensor_reduce(top[:, :], psg, mybir.AxisListType.X, ALU.max).then_inc(route, 1)
                dve.wait_ge(route, base + 1)
                dve.tensor_tensor(lg[:, :, :], psg, top[:, :].unsqueeze(2).broadcast_to([P, CT, E]), ALU.subtract
                                  ).then_inc(route, 1)
                dve.wait_ge(route, base + 2)
                dve.tensor_scalar(pick[:, :, :], lg[:, :, :], 0.0, float(E), ALU.is_lt, ALU.mult).then_inc(route, 1)
                dve.wait_ge(route, base + 3)
                dve.tensor_tensor(pick[:, :, :], pick[:, :, :], iota_e[:, :, :], ALU.add).then_inc(route, 1)
                dve.wait_ge(route, base + 4)
                dve.tensor_reduce(idx[:, :], pick[:, :, :], mybir.AxisListType.X, ALU.min).then_inc(route, 1)
                dve.wait_ge(route, base + 5)
                dve.tensor_tensor(hot[:, :, 1:].rearrange("p e t -> p t e"), iota_e[:, :, :],
                                  idx[:, :].unsqueeze(2).broadcast_to([P, CT, E]), ALU.is_equal).then_inc(route, 1)
                dve.wait_ge(route, base + 6)
                dve.tensor_tensor_scan(run[:, :, :].rearrange("p e t -> p (e t)"), reset[:, :],
                                       hot[:, :, :].rearrange("p e t -> p (e t)"), 0.0, ALU.mult, ALU.add
                                       ).then_inc(route, 1)
                dve.wait_ge(route, base + 7)
                dve.tensor_copy(hot[:, :, 0:1], run[:, :, CT:]).then_inc(route, 1)

            def x1_statistics(k, m, over):
                dve.wait_ge(x1_ready, k + 1)
                statistics(k, bn2_done, mv2_done)

            def normalise_u(k, m, over):
                inverse_std(k, std2_done, rstd2_done)
                if past(k, 3):
                    dve.wait_ge(scattered[m % 3], over(3) * (16 * CT))
                for j in range(CT):
                    dve.tensor_scalar(ut[:, m % 3 * CT + j, 0:C],
                                      xt[:, bass.ds(k * CT + j, 1), :].rearrange("p j c -> p (j c)"),
                                      mv[:, j, 0:1], rstd[:, j:j + 1], ALU.subtract, ALU.mult).then_inc(u_ready, 1)

            def route_b(k, m, over):
                base = k * ROUTE + 8
                dve.wait_ge(counted, k + 1)
                dve.tensor_tensor(place[:, :, :], banks[:, 6, 0:CT * E].rearrange("p (e t) -> p e t", e=E),
                                  hot[:, :, 1:], ALU.mult).then_inc(route, 1)
                dve.wait_ge(route, base + 1)
                dve.tensor_reduce(pos[:, :], place[:, :, :].rearrange("p e t -> p t e"), mybir.AxisListType.X, ALU.add
                                  ).then_inc(route, 1)
                dve.wait_ge(route, base + 2)
                dve.scalar_tensor_tensor(raw_slot[:, :], idx[:, :], float(CAP), pos[:, :], ALU.mult, ALU.add
                                         ).then_inc(route, 1)
                dve.tensor_scalar(over_cap[:, :], pos[:, :], CAP + 0.5, float(1 << 15), ALU.is_gt, ALU.mult
                                  ).then_inc(route, 1)
                dve.wait_ge(route, base + 4)
                dve.scalar_tensor_tensor(slot[m % 3][:, :], raw_slot[:, :], -1.0, over_cap[:, :], ALU.add, ALU.add
                                         ).then_inc(route, 1)
                dve.wait_ge(exp_done, k + 1)
                dve.tensor_reduce(den[:, :], ex[:, :, :], mybir.AxisListType.X, ALU.add).then_inc(route, 1)
                dve.wait_ge(route, base + 6)
                mine = ut[:, m % 3 * CT:m % 3 * CT + CT, :]
                dve.reciprocal(mine[:, :, C:C + 1], den[:, :].unsqueeze(2)).then_inc(route, 1)
                dve.tensor_copy(mine[:, :, C + 1:ROW].bitcast(I32), tok_no[:, bass.ds(k * CT, CT)].unsqueeze(2)
                                ).then_inc(route, 1)

            pipeline(dve, NCH, 6, [(1, gate_value), (2, x1_statistics), (3, route_a), (2, normalise_u), (3, route_b)])

            def x_rest(s, m):
                dve.wait_ge(xe_hi, s + 1)
                dve.tensor_tensor(x_hl[m % 2][:, 1, :, :], banks[:, 5:7, 0:STEP], x_hl[m % 2][:, 0, :, :], ALU.subtract
                                  ).then_inc(xe_lo, 1)

            def rest_h(s, m, f):
                g = s * KF + f
                part = h_hl[(m * KF + f) % 3]
                dve.wait_ge(h_ready, g + 1)
                dve.tensor_tensor(part[:, 1, :], h32[f % 2][:, :], part[:, 0, :], ALU.subtract).then_inc(h_lo, 1)

            def keep_y1(s, m, i):
                dve.wait_ge(step_done, s + 1)
                if past(s, 1):
                    dve.wait_ge(y_turned, s * 2)
                dve.tensor_scalar(y32[:, 1, :], banks[:, 4, 0:STEP],
                                  b2s[:, bass.ds((i * 2 + m // EXPERT_STEPS) * KC + 1, 1)], None, ALU.add
                                  ).then_inc(y1_kept, 1)

            def guard_y(s, m, r):
                y = y_rows[m % 2][:, 2 * r:2 * r + 2, :].rearrange("p j c -> p (j c)")
                base = s * 12 + 6 * r
                dve.wait_ge(y_scaled, s * 2 + r + 1)
                if past(s, 1) or r:
                    dve.wait_ge(y_guard, base)
                dve.tensor_tensor(y_nil[:, :], y, y, ALU.subtract).then_inc(y_guard, 1)
                dve.tensor_scalar(y_fix[:, :], y, FMAX, 1e4, ALU.is_gt, ALU.mult).then_inc(y_guard, 1)
                dve.tensor_scalar(y_neg[:, :], y, -FMAX, -1e4, ALU.is_lt, ALU.mult).then_inc(y_guard, 1)
                dve.wait_ge(y_guard, base + 1)
                dve.tensor_scalar(y_bad[:, :], y_nil[:, :], 0.0, None, ALU.not_equal).then_inc(y_guard, 1)
                dve.wait_ge(y_guard, base + 3)
                dve.tensor_tensor(y_fix[:, :], y_fix[:, :], y_neg[:, :], ALU.add).then_inc(y_guard, 1)
                hold(dve, y_guard, base + 5, held)
                dve.copy_predicated(y, y_bad[:, :], y_fix[:, :]).then_inc(y_guard, 1)

            x_rest(0, 0)

            def pair(i, first, last):
                for m in range(PAIR):
                    s, before = i * PAIR + m, i * PAIR + (m - 1)
                    some = not (first and m == 0)
                    for f in range(KF):
                        rest_h(s, m, f)
                        if f == 2 and some:
                            keep_y1(before, m - 1, i)
                        if f == 4 and some:
                            guard_y(before, m - 1, 0)
                        if f == 5 and not (last and m == PAIR - 1):
                            x_rest(i * PAIR + (m + 1), m + 1)
                        if f == 6 and some:
                            guard_y(before, m - 1, 1)
                if last:
                    keep_y1(STEPS - 1, PAIR - 1, i)
                    for r in range(2):
                        guard_y(STEPS - 1, PAIR - 1, r)

            pair(0, True, False)
            with dve.Fori(1, PAIRS - 1) as i:
                pair(i, False, False)
            pair(PAIRS - 1, False, True)

            def add_y(k, m, over):
                dve.wait_ge(y_loaded[m], over(2) * 16 + 16)
                if past(k, 2):
                    dve.wait_ge(sum_turned, k - 1)
                dve.tensor_tensor(total[m][:, :, :], xt[:, bass.ds(k * CT, CT), :], y_in[m][:, :, :], ALU.add
                                  ).then_inc(summed, 1)

            pipeline(dve, NCH, 2, [(0, add_y)])

        @block.tensor
        def _(pe):
            pe.wait_ge(made, MADE)
            pe.wait_ge(consts_loaded, 16 * CONSTS)
            pe.wait_ge(const_v, CONST_V)

            def to_tokens(bank, src, count=P):
                for j in range(CT):
                    for u in range(KC):
                        last = pe.transpose(tokens_of(bank)[:, j, u * P:(u + 1) * P], src[:, u, j * P:(j + 1) * P],
                                            ident[:, :])
                return last

            def to_planar(bank, src):
                for u in range(KC):
                    for j in range(CT):
                        last = pe.transpose(banks[:, bank + u, j * P:(j + 1) * P], src(j)[:, u * P:(u + 1) * P],
                                            ident[:, :])
                return last

            def turn_x(k, m, over):
                pe.wait_ge(x_loaded[m], over(2) * 16 + 16)
                if past(k, 2):
                    pe.wait_ge(x_kept, k - 1)
                to_tokens(2 * m, work_uc[m]).then_inc(x_turned, 1)

            def turn_f(k, m, over):
                pe.wait_ge(f_ready, k * CT + CT)
                if past(k, 2):
                    pe.wait_ge(f_kept, k - 1)
                to_planar(4 + 2 * m, lambda j: work_jc[2 + m][:, j, :]).then_inc(f_turned, 1)

            pipeline(pe, NCH, 2, [(0, turn_x), (1, turn_f)])

            pe.wait_ge(f_kept, NCH)

            def turn_q(k, m, over):
                pe.wait_ge(scaled, k + 1)
                if past(k, 2):
                    pe.wait_ge(qT_ready, k - 1)
                to_tokens(2 * m, work_uc[2 + m]).then_inc(q_turned, 1)

            def sums(k, m, over):
                pe.wait_ge(qT_ready, k + 1)
                for j in range(CT):
                    for u in range(KC):
                        last = pe.matmul(banks[:, 4 + u, 0:3 * NB], qT[m][:, j, u * P:(u + 1) * P],
                                         basis_f[:, bass.ds(k * CT + j, 1), :].rearrange("p j c -> p (j c)"),
                                         start=isinstance(k, int) and k == 0 and j == 0,
                                         stop=isinstance(k, int) and k == NCH - 1 and j == CT - 1)
                last.then_inc(dft_done, 1)

            pipeline(pe, NCH, 2, [(0, turn_q), (1, sums)])

            pe.wait_ge(coef_steps, 12)
            for r in range(2):
                for u in range(KC):
                    at = (r * KC + u) * P // 2
                    last = pe.transpose(banks[0:3 * PART, 6, at:at + P // 2].bitcast(F16), coef16[:, u, r, :], ident16[:, :])
            last.then_inc(coef_turned, 1)

            def wave(k, m, over):
                pe.wait_ge(basis_loaded[m], over(2) * 16 + 16)
                if past(k, 1):
                    pe.wait_ge(squared, k * 2)
                for r in range(2):
                    for u in range(KC):
                        last = pe.matmul(banks[:, 2 * r + u, :], waves[:, r, u, :], basis_i[m], start=True, stop=True)
                last.then_inc(waved, 1)

            def conv(out_tile, a_hi, a_lo, w, bias):
                n = 0
                for u in range(KC):
                    for a, b in ((a_hi, 0), (a_hi, 1), (a_lo, 0)):
                        pe.matmul(out_tile, a[:, u, :], w[:, b, u, :], start=n == 0, stop=False)
                        n += 1
                return pe.matmul(out_tile, ones2[:, :], bias, start=False, stop=True)

            def query(k, m, over):
                pe.wait_ge(fq_lo, k + 1)
                if past(k, 2):
                    pe.wait_ge(m8_ready, k - 1)
                for j in range(CT):
                    last = conv(tokens_of(4 + 2 * m)[:, j, :], hi[m][:, :, j * P:(j + 1) * P],
                                lo[m][:, :, j * P:(j + 1) * P], wq_hl, biases[:, 0, :])
                last.then_inc(queried, 1)

            pe.wait_ge(waves_ready, 1)
            pipeline(pe, NCH, 2, [(0, wave), (2, query)])

            pe.wait_ge(m8_ready, NCH)
            pe.wait_ge(squared, 2 * NCH)

            def count(k, m, over):
                pe.wait_ge(route, k * ROUTE + 7)
                pe.matmul(banks[:, 6, 0:CT * E], tri[:, :], hot[:, :, 1:], start=True, stop=False)
                pe.matmul(banks[:, 6, 0:CT * E], ones_b[:, :], run[:, :, 0:CT], start=False, stop=True
                          ).then_inc(counted, 1)

            def turn_u(k, m, over):
                pe.wait_ge(u_ready, k * CT + CT)
                if past(k, 1):
                    pe.wait_ge(u_kept, k)
                to_planar(2, lambda j: ut[:, m % 3 * CT + j, 0:C]).then_inc(u_turned, 1)

            def gate_logits(k, m, over):
                pe.wait_ge(u_kept, k + 1)
                if past(k, 2):
                    pe.wait_ge(route, (k - 2) * ROUTE + 2)
                uT = work_uc[2 + m % 2]
                for j in range(CT):
                    o = banks[:, 4 + m % 2, j * E:(j + 1) * E]
                    for u in range(KC):
                        pe.matmul(o, uT[:, u, j * P:(j + 1) * P], gate_col[:, u, :], start=u == 0, stop=False)
                    last = pe.matmul(o, ones1[0:1, :], gb_row[:, :], start=False, stop=True)
                last.then_inc(logits, 1)

            def value(k, m, over):
                pe.wait_ge(v_lo, k + 1)
                if past(k, 1):
                    pe.wait_ge(gated, k)
                for j in range(CT):
                    last = conv(tokens_of(0)[:, j, :], hi[m % 2][:, :, j * P:(j + 1) * P],
                                lo[m % 2][:, :, j * P:(j + 1) * P], wv_hl, biases[:, 1, :])
                last.then_inc(v_done, 1)

            pipeline(pe, NCH, 6, [(3, count), (2, turn_u), (2, gate_logits), (0, value)])

            def turn_rows(s, m, third):
                pe.wait_ge(rows_loaded[m % 3], third)
                if past(s, 1):
                    pe.wait_ge(xe_lo, s)
                for u in range(KC):
                    for j in range(SJ):
                        last = pe.transpose(banks[:, 5 + u, j * SP_:(j + 1) * SP_],
                                            rows[m % 3][:, j, u * P:(u + 1) * P], ident[0:SP_, 0:SP_])
                last.then_inc(rows_turned, 1)

            def up(s, m, f, i):
                g = s * KF + f
                b = m // EXPERT_STEPS
                if f == 0:
                    pe.wait_ge(xe_lo, s + 1)
                    pe.wait_ge(w_lo, (i * 2 + b) * 2 + 1)
                if past(s, 1) or f >= 3:
                    pe.wait_ge(h_ready, g - 2)
                o = banks[:, (m * KF + f) % 3, 0:STEP]
                n = 0
                for u in range(KC):
                    for wp, xp in ((0, 0), (0, 1), (1, 0)):
                        last = pe.matmul(o, w1_hl[b][:, wp, u, f * P:(f + 1) * P], x_hl[m % 2][:, xp, u, :],
                                         start=n == 0, stop=n == 5)
                        n += 1
                last.then_inc(up_done, 1)

            def down(s, m, f, i):
                g = s * KF + f
                b = m // EXPERT_STEPS
                part = h_hl[(m * KF + f) % 3]
                pe.wait_ge(h_lo, g + 1)
                if f == 0:
                    pe.wait_ge(w_lo, (i * 2 + b) * 2 + 2)
                    if past(s, 1):
                        pe.wait_ge(y0_kept, s)
                        pe.wait_ge(y1_kept, s)
                for u in range(KC):
                    for wp, hp in ((0, 0), (0, 1), (1, 0)):
                        last = pe.matmul(banks[:, 3 + u, 0:STEP], w2_hl[b][:, wp, f, u * P:(u + 1) * P], part[:, hp, :],
                                         start=f == 0 and wp + hp == 0, stop=f == KF - 1 and wp == 1)
                last.then_inc(down_done, 1)
                if f == KF - 1:
                    pe.wait_ge(down_done, g + 1)
                    pe.sem_inc(step_done, 1)

            def turn_y(s, m, r):
                if r == 0:
                    pe.wait_ge(y0_kept, s + 1)
                    pe.wait_ge(y1_kept, s + 1)
                if past(s, 1) or r:
                    pe.wait_ge(y_scaled, s * 2 + r)
                for jj in range(2):
                    for u in range(KC):
                        j = 2 * r + jj
                        last = pe.transpose(banks[0:SP_, 7, jj * C + u * P:jj * C + (u + 1) * P],
                                            y32[:, u, j * SP_:(j + 1) * SP_], ident[:, :])
                last.then_inc(y_turned, 1)

            turn_rows(0, 0, 16)

            def pair(i, first, last):
                for m in range(PAIR):
                    for f in range(KF):
                        up(i * PAIR + m, m, f, i)
                        if not (first and m == 0 and f < 2):
                            dm, df = divmod(m * KF + f - 2, KF)
                            down(i * PAIR + dm, dm, df, i)
                        if f in (3, 5) and not (first and m == 0):
                            turn_y(i * PAIR + (m - 1), m - 1, (f - 3) // 2)
                        if f == 4 and not (last and m == PAIR - 1):
                            turn_rows(i * PAIR + (m + 1), m + 1, i * 32 + ((m + 1) // 3 + 1) * 16)
                if last:
                    for f in (KF - 2, KF - 1):
                        down(STEPS - 1, PAIR - 1, f, i)
                    for r in range(2):
                        turn_y(STEPS - 1, PAIR - 1, r)

            pair(0, True, False)
            with pe.Fori(1, PAIRS - 1) as i:
                pair(i, False, False)
            pair(PAIRS - 1, False, True)

            def turn_sum(k, m, over):
                pe.wait_ge(summed, k + 1)
                if past(k, 2):
                    pe.wait_ge(sum_kept, k - 1)
                to_planar(2 * m, lambda j: total[m][:, j, :]).then_inc(sum_turned, 1)

            pipeline(pe, NCH, 2, [(0, turn_sum)])


def waves_tables():
    mirrored = [(0, 1), (1, 0), (1, 1), (1, -1)]
    alone = [(-2, v) for v in (-2, -1, 0, 1)] + [(u, -2) for u in (-1, 0, 1)]
    h, w = np.divmod(np.arange(HW), W)

    def angle(u, v):
        return 2 * np.pi * ((u * h + v * w) % H) / H

    rows = [np.ones(HW)]
    for some in (mirrored, alone):
        rows += [np.cos(angle(u, v)) for u, v in some] + [np.sin(angle(u, v)) for u, v in some]
    table = np.stack(rows)

    def parts(dtype, n):
        left, out = table.copy(), []
        for _ in range(n):
            out.append(left.astype(dtype))
            left = left - out[-1].astype(np.float64)
        return out

    bf16 = mybir.dt.np(BF16)
    fwd = np.concatenate(parts(bf16, 3), 0)
    fwd = np.ascontiguousarray(fwd.T.reshape(NT, P, 3 * NB).transpose(1, 0, 2))
    hi16, lo16 = parts(np.float16, 2)
    inv = np.zeros((3 * PART, HW), np.float16)
    for n, rows16 in enumerate((hi16, hi16, lo16)):
        inv[n * PART:n * PART + NB] = rows16
    return fwd, inv


def kernel(**inputs):
    import concourse.bacc as _bacc
    from concourse.bass_utils import run_bass_kernel_spmd as _run

    a = {n: np.asarray(v) for n, v in inputs.items()}
    fwd, inv = waves_tables()
    f, c = "L0_ffn_", "L0_conv_"
    arrays = {
        "x": a["x"].reshape(C, HW),
        "wqT": a[c + "Wq"].T, "bq": a[c + "bq"].reshape(1, C),
        "wvT": a[c + "Wv"].T, "bv": a[c + "bv"].reshape(1, C),
        "gate_w": a[f + "gate_w"], "gate_b": a[f + "gate_b"].reshape(1, E),
        "w1": a[f + "w1"], "b1T": a[f + "b1"].reshape(E, KF, P).transpose(2, 0, 1).reshape(P, E * KF),
        "w2": a[f + "w2"], "b2T": a[f + "b2"].reshape(E, KC, P).transpose(2, 0, 1).reshape(P, E * KC),
        "fwd": fwd, "inv": inv,
    }
    arrays = {n: np.ascontiguousarray(v) for n, v in arrays.items()}
    nc = _bacc.Bacc("TRN2", target_bir_lowering=False, num_devices=1)
    args = [nc.dram_tensor("in_" + n, v.shape, mybir.dt.from_np(v.dtype), kind="ExternalInput").ap()
            for n, v in arrays.items()]
    out = nc.dram_tensor("out_0_dram", (C, HW), F32, kind="ExternalOutput").ap()
    program(nc, *args, out)
    r = _run(nc, [{"in_" + n: v for n, v in arrays.items()}], core_ids=[0])
    return r.results[0]["out_0_dram"].reshape(1, C, H, W)
```

```python
from contextlib import ExitStack

import numpy as np

import concourse.bass as bass
from concourse import mybir

F32 = mybir.dt.float32
F32R = mybir.dt.float32r
F16 = mybir.dt.float16
BF16 = mybir.dt.bfloat16
I32 = mybir.dt.int32
ALU = mybir.AluOpType
ACT = mybir.ActivationFunctionType
AXX = mybir.AxisListType.X

C, H, W = 256, 96, 96
HW = H * W
P = 128
KC = C // P
NT = HW // P
CT = 4
CHUNK = CT * P
NCH = HW // CHUNK
E, FF = 8, 1024
KF = FF // P
CAP = 1440
SLOTS = E * CAP
STEP = 480
SP_ = 120
SJ = STEP // SP_
STEPS = SLOTS // STEP
EXPERT_STEPS = CAP // STEP
ROW = C + E + 1
NO = C + E
ROWS = 12288
BLANK = 12
NOWHERE = 1 << 20
PERIOD = 24576 // P
NB = 23
NSYM = 9
PART = 32
ROUND = 12582912.0
SLACK = 0.5 - 2.0 ** -14
FMAX = 3.4028234663852886e38


def hold(eng, semaphore, n, held):
    eng.wait_ge(semaphore, n)
    if not isinstance(n, int):
        eng.sem_inc(held, 1)


def past(k, n):
    return not isinstance(k, int) or k >= n


def pipeline(eng, n, turn, stages):
    longest = max(lag for lag, _ in stages)
    head = -(-(longest + 2) // turn)

    def fixed(s):
        for lag, stage in stages:
            k = s - lag
            if 0 <= k < n:
                stage(k, k % turn, lambda d, k=k: k // d)

    for s in range(head * turn):
        fixed(s)
    with eng.Fori(head, n // turn) as i:
        for q in range(turn):
            for lag, stage in stages:
                stage(i * turn + (q - lag), (q - lag) % turn,
                      lambda d, q=q, lag=lag: i * (turn // d) + (q - lag) // d)
    for s in range(n, n + longest):
        fixed(s)


def program(nc, x, wT, b_qv, gate_w, gate_b, w1, w2, b12T, fwd, inv, out):
    ctx = ExitStack()
    with ctx:
        def sem(name):
            return ctx.enter_context(nc.semaphore(name))

        def sb(name, shape, dt, where=ctx):
            return where.enter_context(nc.sbuf_tensor(name, shape, dt))

        slot_rows = nc.dram_tensor("slot_rows", (ROWS, ROW), F32, kind="Internal").ap()
        token_y = nc.dram_tensor("token_y", (HW, C), F32, kind="Internal").ap()

        xt = sb("xt", [P, NT, C], F32)
        ident = sb("ident", [P, P], F32)
        gate_col = sb("gate_col", [P, KC, E], F32)
        b12s = sb("b12s", [P, E * (KF + KC)], F32)
        b1s, b2s = b12s[:, 0:E * KF], b12s[:, E * KF:]
        spare = sb("spare", [P, 2], F32)

        one = ExitStack()
        fc = sb("fc", [P, KC, HW], F32, one)
        query_scope = ExitStack()
        wq_hl = sb("wq_hl", [P, 2, KC, C], F32R, query_scope)
        query_scope.close()
        gate1 = sb("gate1", [P, 2 * KC * C], F32, one)
        wv_hl = sb("wv_hl", [P, 2, KC, C], F32R, one)
        biases = sb("biases", [2, 2, C], F32R, one)
        ones2 = sb("ones2", [2, P], F32R, one)
        bias_scope = ExitStack()
        bias_raw = sb("bias_raw", [2, 2, C], F32, bias_scope)
        bias_hi = sb("bias_hi", [2, 2, C], F32R, bias_scope)
        bias_scope.close()
        m8 = sb("m8", [P, E * NT], F32, one)
        pick = sb("pick", [P, CT, E], F32, one)
        place = sb("place", [P, E, CT], F32, one)
        waves = sb("waves", [3 * PART, 2, KC, P], F16, one)
        run = sb("run", [P, E, CT + 1], BF16, one)
        top, idx, pos, raw_slot, over_cap = (sb(n, [P, CT], F32, one) for n in
                                                  ("top", "idx", "pos", "raw_slot", "over_cap"))
        slot = [sb(f"slot{b}", [P, CT], I32, one) for b in range(3)]
        mv = [sb(f"mv{b}", [P, CT, 2], F32, one) for b in range(2)]
        sb("bias_gap", [P, 60], F32, one)
        sums_scope = ExitStack()
        basis_f = sb("basis_f", [P, NT, 3 * NB], BF16, sums_scope)
        qT = [sb(f"qT{b}", [P, CT, C], BF16, sums_scope) for b in range(2)]
        dft = sb("dft", [P, KC, 3 * NB], F32, sums_scope)
        coef = sb("coef", [P, KC, 2, NB], F32, sums_scope)
        coef16 = sb("coef16", [P, KC, 2, 3 * PART], F16, sums_scope)
        most = sb("most", [P, KC, NCH], F32, sums_scope)
        least = sb("least", [P, KC, NCH], F32, sums_scope)
        sums_scope.close()
        hi = [sb(f"hi{b}", [P, KC, CHUNK], F32R, one) for b in range(2)]
        lo = [sb(f"lo{b}", [P, KC, CHUNK], F32R, one) for b in range(2)]
        work = [sb(f"work{b}", [P, 1024], F32, one) for b in range(4)]
        ut = sb("ut", [P, 3 * CT, ROW], F32, one)
        ident16 = sb("ident16", [P, P], F16, one)
        bn6 = sb("bn6", [P, CT, 6], F32, one)
        rstd = [sb(f"rstd{b}", [P, CT], F32, one) for b in range(2)]
        shift = [sb(f"shift{b}", [P, CT], F32, one) for b in range(2)]
        eps = sb("eps", [P, 2], F32, one)
        std = [sb(f"std{b}", [P, CT], F32, one) for b in range(2)]
        qs = sb("qs", [P, 6, KC], F32, one)
        gb_row = sb("gb_row", [1, CT * E], F32, one)
        ones1 = sb("ones1", [2, P], F32, one)
        tri = sb("tri", [P, P], BF16, one)
        ones_b = sb("ones_b", [P, P], BF16, one)
        iota_e = sb("iota_e", [P, CT, E], F32, one)
        tok_no = sb("tok_no", [P, NT], I32, one)
        reset = sb("reset", [P, E * (CT + 1)], F32, one)
        hot = sb("hot", [P, E, CT + 1], BF16, one)
        one.close()

        PAIR = 2 * EXPERT_STEPS

        two = ExitStack()
        w_raw = sb("w_raw", [P, KC * FF], F32, two)
        w1_hl, w2_hl = [], []
        for b in range(2):
            w1_hl.append(sb(f"w1_hl{b}", [P, 2, KC, FF], F32R, two))
            w2_hl.append(sb(f"w2_hl{b}", [P, 2, KF, C], F32R, two))
        rows = [sb(f"rows{b}", [SP_, SJ, ROW], F32, two) for b in range(3)]
        x_hl = [sb(f"x_hl{b}", [P, 2, KC, STEP], F32R, two) for b in range(2)]
        h32 = [sb(f"h32_{b}", [P, STEP], F32, two) for b in range(2)]
        h_hl = [sb(f"h_hl{b}", [P, 2, STEP], F32R, two) for b in range(4)]
        y32 = sb("y32", [P, KC, STEP], F32, two)
        y_bad = sb("y_bad", [SP_, 2 * C], I32, two)
        y_fix = sb("y_fix", [SP_, 2 * C], F32, two)
        ex = sb("ex", [SP_, SJ, E], F32, two)
        den = sb("den", [SP_, SJ], F32, two)
        prob = [sb(f"prob{b}", [SP_, SJ], F32, two) for b in range(PAIR)]
        number = [sb(f"number{b}", [SP_, SJ], I32, two) for b in range(PAIR)]
        y_rows = [sb(f"y_rows{b}", [SP_, SJ, C], F32, two) for b in range(2)]
        two.close()

        three = ExitStack()
        y_in = [sb(f"y_in{b}", [P, CT, C], F32, three) for b in range(6)]
        total = [sb(f"total{b}", [P, CT, C], F32, three) for b in range(3)]
        planar = [sb(f"planar{b}", [P, KC, CHUNK], F32, three) for b in range(3)]
        three.close()

        banks = ctx.enter_context(nc.psum_tensor("banks", [P, 8, 512], F32))

        def tokens_of(bank):
            return banks[:, bank:bank + 2, :].rearrange("p u (v c) -> p (u v) c", c=C)

        consts_loaded = sem("consts_loaded")
        tables_loaded = sem("tables_loaded")
        made = sem("made")
        spared = sem("spared")
        blanks = sem("blanks")
        x_turned = sem("x_turned")
        x_kept = sem("x_kept")
        bn_done = sem("bn_done")
        mv_done = sem("mv_done")
        rstd_done = sem("rstd_done")
        std_done = sem("std_done")
        std2_done = sem("std2_done")
        held = sem("held")
        shift_done = sem("shift_done")
        shift2_done = sem("shift2_done")
        f_ready = sem("f_ready")
        f_turned = sem("f_turned")
        f_kept = sem("f_kept")
        ranged = sem("ranged")
        range_steps = sem("range_steps")
        magnitudes = sem("magnitudes")
        scaled = sem("scaled")
        q_turned = sem("q_turned")
        qT_ready = sem("qT_ready")
        dft_done = sem("dft_done")
        coef_steps = sem("coef_steps")
        coef_turned = sem("coef_turned")
        waves_ready = sem("waves_ready")
        waved = sem("waved")
        squared = sem("squared")
        power_ready = sem("power_ready")
        root_ready = sem("root_ready")
        fq_hi = sem("fq_hi")
        fq_lo = sem("fq_lo")
        queried = sem("queried")
        m8_ready = sem("m8_ready")
        gate_steps = sem("gate_steps")
        v_hi = sem("v_hi")
        v_lo = sem("v_lo")
        v_done = sem("v_done")
        gated = sem("gated")
        x1_ready = sem("x1_ready")
        bn2_done = sem("bn2_done")
        mv2_done = sem("mv2_done")
        rstd2_done = sem("rstd2_done")
        u_ready = sem("u_ready")
        u_turned = sem("u_turned")
        u_kept = sem("u_kept")
        logits = sem("logits")
        routed = sem("routed")
        placed = sem("placed")
        exp_done = sem("exp_done")
        counted = sem("counted")
        w1_loaded = sem("w1_loaded")
        w2_loaded = sem("w2_loaded")
        w_hi = sem("w_hi")
        w_lo = sem("w_lo")
        rows_turned = sem("rows_turned")
        xe_hi = sem("xe_hi")
        xe_lo = sem("xe_lo")
        up_done = sem("up_done")
        h_ready = sem("h_ready")
        h_lo = sem("h_lo")
        down_done = sem("down_done")
        step_done = sem("step_done")
        y0_kept = sem("y0_kept")
        y1_kept = sem("y1_kept")
        y_turned = sem("y_turned")
        y_scaled = sem("y_scaled")
        den_done = sem("den_done")
        prob_done = sem("prob_done")
        y_guard = sem("y_guard")
        summed = sem("summed")
        sum_turned = sem("sum_turned")
        sum_kept = sem("sum_kept")
        const_v = sem("const_v")
        x_loaded = [sem(f"x_loaded{b}") for b in range(2)]
        basis_loaded = [sem(f"basis_loaded{b}") for b in range(2)]
        scattered = [sem(f"scattered{b}") for b in range(3)]
        rows_loaded = [sem(f"rows_loaded{b}") for b in range(3)]
        y_out = [sem(f"y_out{b}") for b in range(2)]
        y_loaded = [sem(f"y_loaded{b}") for b in range(6)]
        stored = [sem(f"stored{b}") for b in range(3)]

        W_PARTS = 4
        W_PART = KC * FF // W_PARTS
        W_SLOTS = [(0, f) for f in (4, 5, 6, 7)] + [(2, f) for f in (0, 1, 2, 3)]
        PAIRS = E // 2
        WARM0, WARM1 = 14, 4
        work_uc = [t[:, :].rearrange("p (u n) -> p u n", u=KC) for t in work]
        work_jc = [t[:, :].rearrange("p (j c) -> p j c", j=CT) for t in work]
        im_sq = [ut[:, 4 * b:4 * b + 4, :].rearrange("p a c -> p (a c)")[:, 0:1024] for b in range(2)]
        basis_i = [ut[0:3 * PART, 8 + b, 0:CHUNK // 2].bitcast(F16) for b in range(2)]
        blank = ut[:, 11:12, :]
        w_qv = ut[:, 0:4, :].rearrange("p a c -> p (a c)")[:, 0:2 * KC * C].rearrange("p (u o) -> p u o", u=KC)
        gate_out = banks[:, 6, 0:CT * E].rearrange("p (t e) -> p t e", e=E)
        MADE, CONSTS, TABLES, CONST_V, ROUTED, PLACED = 11, 2, 4, 8, 8, 6
        BLANKS = (ROWS // P + NT) // BLANK
        block = ctx.enter_context(nc.Block())

        @block.sync
        def _(sp):
            def load_x(k, m, over):
                if past(k, 2):
                    hold(sp, x_turned, k - 1, held)
                sp.dma_start(work_uc[m][:, :, :], x.rearrange("(u p) n -> p u n", p=P)[:, :, bass.ds(k * CHUNK, CHUNK)]
                             ).then_inc(x_loaded[m], 16)

            pipeline(sp, NCH, 2, [(0, load_x)])
            sp.dma_start(basis_f[:, :, :], fwd).then_inc(tables_loaded, 16)

            def load_basis(k, m, over):
                if past(k, 2):
                    hold(sp, waved, k - 1, held)
                sp.dma_start(basis_i[m], inv[:, bass.ds(k * CHUNK, CHUNK)]).then_inc(basis_loaded[m], 16)

            pipeline(sp, NCH, 2, [(0, load_basis)])

            def load_w1(e):
                if past(e, 1):
                    hold(sp, w_lo, e * 2, held)
                sp.dma_start(w_raw[:, :].rearrange("p (u f) -> p u f", u=KC),
                             w1[bass.ds(e, 1), :, :].rearrange("e (u p) f -> p (e u) f", p=P)).then_inc(w1_loaded, 16)

            def load_w2(e):
                hold(sp, w_lo, e * 2 + 1, held)
                sp.dma_start(w_raw[:, :].rearrange("p (u c) -> p u c", u=KF),
                             w2[bass.ds(e, 1), :, :].rearrange("e (u p) c -> p (e u) c", p=P)).then_inc(w2_loaded, 16)

            sp.wait_ge(v_lo, CT)
            load_w1(0)
            load_w2(0)

            sp.wait_ge(placed, PLACED * NCH)
            sp.wait_ge(logits, NCH)
            for m in range(3):
                sp.wait_ge(scattered[m], 16 * CT * NCH // 3)

            def load_rows(s, m):
                if past(s, 3):
                    hold(sp, prob_done, s - 2, held)
                sp.dma_start(rows[m % 3][:, :, :],
                             slot_rows[bass.ds(s * STEP, STEP), :].rearrange("(j p) c -> p j c", p=SP_)
                             ).then_inc(rows_loaded[m % 3], 16)

            load_rows(0, 0)
            load_rows(1, 1)

            def pair(i, first, last):
                for m in range(PAIR):
                    if m % EXPERT_STEPS == 0 and not (last and m):
                        load_w1(i * 2 + m // EXPERT_STEPS + 1)
                    if not (last and m + 2 >= PAIR):
                        load_rows(i * PAIR + m + 2, m + 2)
                    if m % EXPERT_STEPS == 0 and not (last and m):
                        load_w2(i * 2 + m // EXPERT_STEPS + 1)

            pair(0, True, False)
            with sp.Fori(1, PAIRS - 1) as i:
                pair(i, False, False)
            pair(PAIRS - 1, False, True)

            for b in range(2):
                sp.wait_ge(y_out[b], 16 * SJ * STEPS // 2)

            def load_y(k, m, over):
                if past(k, 6):
                    hold(sp, summed, k - 5, held)
                sp.dma_start(y_in[m][:, :, :],
                             token_y[bass.ds(k * CHUNK, CHUNK), :].rearrange("(j p) c -> p j c", p=P)
                             ).then_inc(y_loaded[m], 16)

            pipeline(sp, NCH, 6, [(0, load_y)])
            for b in range(3):
                sp.wait_ge(stored[b], 16 * NCH // 3)

        @block.gpsimd
        def _(pool):
            pool.memset(ident[:, :], 0.0).then_inc(made, 1)
            pool.memset(ident16[:, :], 0.0).then_inc(made, 1)
            pool.memset(tri[:, :], 1.0).then_inc(made, 1)
            pool.memset(blank[:, :, :], 0.0).then_inc(made, 1)
            pool.memset(reset[:, :], 1.0).then_inc(made, 1)
            pool.memset(ones_b[:, :], 1.0)
            pool.memset(ones1[:, :], 1.0)
            pool.memset(eps[:, 0:1], 1e-6)
            pool.memset(eps[:, 1:2], 1e-5)
            pool.memset(hot[:, :, :], 0.0)
            pool.memset(coef16[:, :, :, :], 0.0)
            pool.iota(iota_e[:, :, :], pattern=[[0, CT], [1, E]], base=0, channel_multiplier=0,
                      allow_small_or_imprecise_dtypes=True)
            pool.iota(tok_no[:, :], pattern=[[P, NT]], base=0, channel_multiplier=1).then_inc(made, 1)
            pool.wait_ge(made, 6)
            for m in (ident, ident16):
                pool.affine_select(out=m[:, :], in_=m[:, :], compare_op=ALU.not_equal, fill=1.0, base=0,
                                   pattern=[[-1, P]], channel_multiplier=1).then_inc(made, 1)
            pool.affine_select(out=tri[:, :], in_=tri[:, :], compare_op=ALU.is_ge, fill=0.0, base=0,
                               pattern=[[1, P]], channel_multiplier=-1).then_inc(made, 1)
            pool.memset(blank[:, :, NO:ROW].bitcast(I32), NOWHERE).then_inc(made, 1)
            pool.memset(reset[:, :].rearrange("p (e t) -> p e t", e=E)[:, :, 0:1], 0.0).then_inc(made, 1)

            pool.wait_ge(made, MADE)
            pool.wait_ge(x_turned, NCH - 2)
            for q in range(ROWS // P // BLANK):
                pool.dma_start(slot_rows.rearrange("(p r) c -> p r c", p=P)[:, q * BLANK:(q + 1) * BLANK, :],
                               blank[:, :, :].broadcast_to([P, BLANK, ROW])).then_inc(blanks, 16)
            for q in range(NT // BLANK):
                pool.dma_start(token_y.rearrange("(p r) c -> p r c", p=P)[:, q * BLANK:(q + 1) * BLANK, :],
                               blank[:, :, 0:C].broadcast_to([P, BLANK, C])).then_inc(blanks, 16)

            def power(k, m, over):
                hold(pool, squared, k * 2 + 2, held)
                if past(k, 2):
                    hold(pool, fq_lo, k - 1, held)
                pool.tensor_tensor(work[2 + m][:, :], work[m][:, :], im_sq[m][:, :], ALU.add).then_inc(power_ready, 1)

            pipeline(pool, NCH, 2, [(0, power)])

            pool.wait_ge(blanks, 16 * BLANKS)

            def rest(k, m, over):
                hold(pool, v_hi, k + 1, held)
                pool.tensor_tensor(lo[m % 2][:, :, :], fc[:, :, bass.ds(k * CHUNK, CHUNK)],
                                   hi[m % 2][:, :, :], ALU.subtract).then_inc(v_lo, 1)

            def scatter(k, m, over):
                hold(pool, placed, k * PLACED + PLACED, held)
                for j in range(CT):
                    pool.indirect_dma_start(
                        out=slot_rows[:, :], out_offset=bass.IndirectOffsetOnAxis(slot[m % 3][:, j:j + 1], 0),
                        in_=ut[:, m % 3 * CT + j, :], in_offset=None, bounds_check=SLOTS - 1, oob_is_err=False,
                    ).then_inc(scattered[m % 3], 16)

            pipeline(pool, NCH, 6, [(5, scatter), (0, rest)])

            def rest_w(e, b, n):
                hold(pool, w_hi, e * (2 * W_PARTS) + (n + 1) * W_PARTS, held)
                hl = (w1_hl, w2_hl)[n][b][:, :, :, :].rearrange("p a u c -> p a (u c)")
                pool.tensor_tensor(hl[:, 1, :], w_raw[:, :], hl[:, 0, :], ALU.subtract).then_inc(w_lo, 1)

            def scatter_y(s, m):
                for r in range(2):
                    hold(pool, y_guard, s * 12 + 6 * r + 6, held)
                    for j in (2 * r, 2 * r + 1):
                        pool.indirect_dma_start(
                            out=token_y[:, :],
                            out_offset=bass.IndirectOffsetOnAxis(number[m % PAIR][:, j:j + 1], 0),
                            in_=y_rows[m % 2][:, j, :], in_offset=None, bounds_check=HW - 1, oob_is_err=False,
                        ).then_inc(y_out[m % 2], 16)

            def pair(i, first, last):
                for m in range(PAIR):
                    weights = not (last and m >= EXPERT_STEPS)
                    if m % EXPERT_STEPS == 2 and weights:
                        rest_w(i * 2 + m // EXPERT_STEPS + 1, (m // EXPERT_STEPS + 1) % 2, 1)
                    if not (first and m == 0):
                        scatter_y(i * PAIR + (m - 1), m - 1)
                    if m % EXPERT_STEPS == 0 and weights:
                        rest_w(i * 2 + m // EXPERT_STEPS + 1, (m // EXPERT_STEPS + 1) % 2, 0)
                if last:
                    scatter_y(STEPS - 1, PAIR - 1)

            pair(0, True, False)
            with pool.Fori(1, PAIRS - 1) as i:
                pair(i, False, False)
            pair(PAIRS - 1, False, True)

        @block.scalar
        def _(act):
            for dst, src in ((w_qv, wT.rearrange("(u p) o -> p u o", p=P)), (bias_raw[:, :, :], b_qv)):
                act.dma_start(dst, src).then_inc(consts_loaded, 16)
            for dst, src in ((gate_col[:, :, :], gate_w.rearrange("(u p) e -> p u e", p=P)), (b12s[:, :], b12T),
                             (gb_row[:, :], gate_b)):
                act.dma_start(dst, src).then_inc(tables_loaded, 16)
            act.wait_ge(made, MADE)
            act.activation(spare[:, :], eps[:, :], ACT.Sqrt).then_inc(spared, 1)

            def keep_x(k, m, over):
                hold(act, x_turned, k + 1, held)
                act.activation(xt[:, bass.ds(k * CT, CT), :], tokens_of(2 * m), ACT.Copy).then_inc(x_kept, 1)

            def keep_f(k, m, over):
                hold(act, f_turned, k + 1, held)
                act.activation(fc[:, :, bass.ds(k * CHUNK, CHUNK)], banks[:, 4 + 2 * m:6 + 2 * m, :], ACT.Copy
                               ).then_inc(f_kept, 1)

            def deviation(k, b, n, variances, done, used):
                if past(k, 2):
                    hold(act, used, k - 1, held)
                hold(act, variances, k * CT + CT, held)
                act.activation(std[b][:, :], mv[b][:, :, 1], ACT.Sqrt, bias=eps[:, n:n + 1]).then_inc(done, 1)

            def normalise(k, b, tile):
                for j in range(CT):
                    last = act.activation(tile(j), xt[:, bass.ds(k * CT + j, 1), :].rearrange("p j c -> p (j c)"),
                                          ACT.Identity, bias=shift[b][:, j:j + 1], scale=rstd[b][:, j:j + 1])
                return last

            def x_normalised(k, m, over):
                hold(act, shift_done, k + 1, held)
                if past(k, 2):
                    hold(act, f_turned, k - 1, held)
                normalise(k, m, lambda j: work_jc[2 + m][:, j, :]).then_inc(f_ready, 1)

            def x_deviation(k, m, over):
                deviation(k, m, 0, mv_done, std_done, rstd_done)

            pipeline(act, NCH, 2, [(0, keep_x), (1, x_deviation), (2, keep_f), (1, x_normalised)])

            act.wait_ge(ranged, NCH)

            def magnitude(k, m, over):
                if past(k, 2):
                    hold(act, scaled, k - 1, held)
                act.activation(work_uc[m][:, :, :], fc[:, :, bass.ds(k * CHUNK, CHUNK)], ACT.Abs
                               ).then_inc(magnitudes, 1)

            pipeline(act, NCH, 2, [(0, magnitude)])

            def square(k, m, over):
                hold(act, waved, k + 1, held)
                act.activation(work_uc[m][:, :, :], banks[:, 0:2, :], ACT.Square).then_inc(squared, 1)
                act.activation(im_sq[m][:, :].rearrange("p (u n) -> p u n", u=KC), banks[:, 2:4, :], ACT.Square
                               ).then_inc(squared, 1)

            def root(k, m, over):
                hold(act, power_ready, k + 1, held)
                act.activation(work[2 + m][:, :], work[2 + m][:, :], ACT.Sqrt).then_inc(root_ready, 1)

            pipeline(act, NCH, 2, [(0, square), (1, root)])

            def value_hi(k, m, over):
                if past(k, 2):
                    hold(act, v_done, k - 1, held)
                else:
                    act.wait_ge(queried, NCH - 1 + k)
                act.activation(hi[m % 2][:, :, :], fc[:, :, bass.ds(k * CHUNK, CHUNK)], ACT.Copy).then_inc(v_hi, 1)

            def u_normalised(k, m, over):
                hold(act, shift2_done, k + 1, held)
                if past(k, 3):
                    hold(act, scattered[m % 3], over(3) * (16 * CT), held)
                normalise(k, m % 2, lambda j: ut[:, m % 3 * CT + j, 0:C]).then_inc(u_ready, 1)

            def keep_u(k, m, over):
                hold(act, u_turned, k + 1, held)
                act.activation(work_uc[2 + m % 2][:, :, :], banks[:, 4:6, :], ACT.Copy).then_inc(u_kept, 1)

            def round_w(e, b, n):
                if n == 0 and past(e, 2):
                    hold(act, step_done, (e - 1) * EXPERT_STEPS, held)
                if n % W_PARTS == 0:
                    hold(act, (w1_loaded, w2_loaded)[n // W_PARTS], e * 16 + 16, held)
                hl = (w1_hl, w2_hl)[n // W_PARTS][b][:, :, :, :].rearrange("p a u c -> p a (u c)")
                part = slice(n % W_PARTS * W_PART, (n % W_PARTS + 1) * W_PART)
                act.activation(hl[:, 0, part], w_raw[:, part], ACT.Copy).then_inc(w_hi, 1)

            def first_w1(k, m, over):
                if isinstance(k, int) and NCH - 3 <= k < NCH - 1:
                    for n in range(W_PARTS // 2):
                        round_w(0, 0, (k - (NCH - 3)) * (W_PARTS // 2) + n)

            def x1_deviation(k, m, over):
                deviation(k, m % 2, 1, mv2_done, std2_done, rstd2_done)

            pipeline(act, NCH, 6, [(0, value_hi), (3, u_normalised), (3, keep_u), (3, first_w1), (2, x1_deviation)])

            def x_rounded(s, m):
                if past(s, 1):
                    hold(act, den_done, s, held)
                hold(act, rows_turned, s + 1, held)
                act.activation(x_hl[m % 2][:, 0, :, :], banks[:, 5:7, 0:STEP], ACT.Copy).then_inc(xe_hi, 1)
                act.activation(ex[:, :, :], rows[m % 3][:, :, C:NO], ACT.Exp).then_inc(exp_done, 1)

            def hidden(s, m, f, i):
                g = s * KF + f
                hold(act, up_done, g + 1, held)
                if past(s, 1) or f >= 2:
                    hold(act, h_lo, g - 1, held)
                if past(s, 1) or f >= 4:
                    hold(act, down_done, g - 3, held)
                bias = b1s[:, bass.ds((i * 2 + m // EXPERT_STEPS) * KF + f, 1)]
                part = banks[:, (m * KF + f) % 3, 0:STEP]
                act.activation(h_hl[f % 4][:, 0, :], part, ACT.Relu, bias=bias)
                act.activation(h32[f % 2][:, :], part, ACT.Relu, bias=bias).then_inc(h_ready, 1)

            def keep_y0(s, m, i):
                hold(act, step_done, s + 1, held)
                if past(s, 1):
                    hold(act, y_turned, s * 2, held)
                act.activation(y32[:, 0, :], banks[:, 3, 0:STEP], ACT.Identity,
                               bias=b2s[:, bass.ds((i * 2 + m // EXPERT_STEPS) * KC, 1)]).then_inc(y0_kept, 1)

            def scale_y(s, m, r, left):
                if past(s, 2) and r == 0:
                    hold(act, y_out[m % 2], left, held)
                hold(act, y_turned, s * 2 + r + 1, held)
                hold(act, prob_done, s + 1, held)
                for jj in range(2):
                    j = 2 * r + jj
                    last = act.activation(y_rows[m % 2][:, j, :], banks[0:SP_, 7, jj * C:(jj + 1) * C], ACT.Copy,
                                          scale=prob[m % PAIR][:, j:j + 1])
                last.then_inc(y_scaled, 1)

            act.wait_ge(spared, 1)
            act.activation(spare[:, :], spare[:, :], ACT.Exp).then_inc(spared, 1)
            for n in range(W_PARTS, 2 * W_PARTS):
                round_w(0, 0, n)
            x_rounded(0, 0)

            def pair(i, first, last):
                for m in range(PAIR):
                    s = i * PAIR + m
                    for f in range(KF):
                        if f == 3 and not (first and m == 0):
                            keep_y0(i * PAIR + (m - 1), m - 1, i)
                        hidden(s, m, f, i)
                        if not (last and m >= EXPERT_STEPS) and (m % EXPERT_STEPS, f) in W_SLOTS:
                            round_w(i * 2 + m // EXPERT_STEPS + 1, (m // EXPERT_STEPS + 1) % 2,
                                    W_SLOTS.index((m % EXPERT_STEPS, f)))
                        if f == 3 and not (last and m == PAIR - 1):
                            x_rounded(i * PAIR + (m + 1), m + 1)
                        if f in (4, 6) and not (first and m == 0):
                            scale_y(i * PAIR + (m - 1), m - 1, (f - 4) // 2,
                                    i * (3 * SJ * 16) + SJ * 16 * ((m - 1) // 2))
                if last:
                    keep_y0(STEPS - 1, PAIR - 1, i)
                    for r in range(2):
                        scale_y(STEPS - 1, PAIR - 1, r, 16 * SJ * ((STEPS - 1) // 2))

            pair(0, True, False)
            with act.Fori(1, PAIRS - 1) as i:
                pair(i, False, False)
            pair(PAIRS - 1, False, True)

            def keep_sum(k, m, over):
                hold(act, sum_turned, k + 1, held)
                if past(k, 3):
                    hold(act, stored[m], over(3) * 16, held)
                act.activation(planar[m][:, :, :], banks[:, 2 * m:2 * m + 2, :], ACT.Copy).then_inc(sum_kept, 1)

            def store(k, m, over):
                hold(act, sum_kept, k + 1, held)
                act.dma_start(out.rearrange("(u p) n -> p u n", p=P)[:, :, bass.ds(k * CHUNK, CHUNK)],
                              planar[m][:, :, :]).then_inc(stored[m], 16)

            pipeline(act, NCH, 3, [(0, keep_sum), (0, store)])

        @block.vector
        def _(dve):
            def sums_of(k, j, done):
                dve.bn_stats(bn6[:, j, :], xt[:, bass.ds(k * CT + j, 1), :].rearrange("p j c -> p (j c)")
                             ).then_inc(done, 1)

            def gather(k, b, summed_up, done):
                hold(dve, summed_up, k * CT + CT, held)
                for j in range(CT):
                    dve.bn_aggr(mv[b][:, j, :], bn6[:, j, :]).then_inc(done, 1)

            def inverse(k, b, std_sem, rstd_sem, used):
                dve.wait_ge(std_sem, k + 1)
                if past(k, 2):
                    dve.wait_ge(used, k - 1)
                dve.reciprocal(rstd[b][:, :], std[b][:, :]).then_inc(rstd_sem, 1)

            def offset(k, b, rstd_sem, shift_sem):
                dve.wait_ge(rstd_sem, k + 1)
                dve.scalar_tensor_tensor(shift[b][:, :], mv[b][:, :, 0], -1.0, rstd[b][:, :], ALU.mult, ALU.mult
                                         ).then_inc(shift_sem, 1)

            def x_sums(k, m, over):
                dve.wait_ge(x_kept, k + 1)
                if past(k, 1):
                    hold(dve, mv_done, k * CT, held)
                for j in range(CT):
                    sums_of(k, j, bn_done)

            def x_gather(k, m, over):
                if past(k, 2):
                    hold(dve, shift_done, k - 1, held)
                gather(k, m, bn_done, mv_done)

            def x_inverse(k, m, over):
                inverse(k, m, std_done, rstd_done, f_ready)

            def x_offset(k, m, over):
                offset(k, m, rstd_done, shift_done)

            def greatest(k, m, over):
                dve.wait_ge(f_kept, k + 1)
                dve.tensor_reduce(most[:, :, bass.ds(k, 1)], fc[:, :, bass.ds(k * CHUNK, CHUNK)], AXX, ALU.max,
                                  apply_absolute_value=True)

            def smallest(k, m, over):
                dve.tensor_reduce(least[:, :, bass.ds(k, 1)], fc[:, :, bass.ds(k * CHUNK, CHUNK)], AXX, ALU.min,
                                  apply_absolute_value=True).then_inc(ranged, 1)

            def split_biases(k, m, over):
                if isinstance(k, int) and k == 0:
                    dve.wait_ge(consts_loaded, 16 * CONSTS)
                    dve.tensor_copy(bias_hi[:, :, :], bias_raw[:, :, :]).then_inc(const_v, 1)
                    dve.wait_ge(const_v, 1)
                    dve.tensor_tensor(biases[:, :, :], bias_raw[:, :, :], bias_hi[:, :, :], ALU.subtract
                                      ).then_inc(const_v, 1)
                    dve.wait_ge(const_v, 2)
                    dve.tensor_copy(biases[0:1, :, :], bias_hi[0:1, :, :]).then_inc(const_v, 1)
                    dve.wait_ge(made, MADE)
                    dve.tensor_copy(ones2[:, :], ones1[:, :]).then_inc(const_v, 1)
                    dve.wait_ge(const_v, 4)

            pipeline(dve, NCH, 2, [(1, split_biases), (1, x_sums), (3, greatest), (1, x_gather), (3, smallest),
                                   (1, x_inverse), (1, x_offset)])

            dve.wait_ge(ranged, NCH)
            dve.tensor_reduce(qs[:, 0, :], most[:, :, :], AXX, ALU.max).then_inc(range_steps, 1)
            dve.tensor_reduce(qs[:, 1, :], least[:, :, :], AXX, ALU.min).then_inc(range_steps, 1)
            dve.wait_ge(range_steps, 2)
            dve.tensor_tensor(qs[:, 2, :], qs[:, 0, :], qs[:, 1, :], ALU.subtract).then_inc(range_steps, 1)
            dve.wait_ge(range_steps, 3)
            dve.reciprocal(qs[:, 3, :], qs[:, 2, :]).then_inc(range_steps, 1)
            dve.scalar_tensor_tensor(qs[:, 5, :], qs[:, 2, :], SLACK / 255.0, qs[:, 1, :], ALU.mult, ALU.add
                                     ).then_inc(range_steps, 1)
            dve.wait_ge(range_steps, 5)
            dve.tensor_scalar(qs[:, 4, :], qs[:, 3, :], 255.0, None, ALU.mult).then_inc(range_steps, 1)
            dve.wait_ge(range_steps, 6)

            def scale_f(k, m, over):
                dve.wait_ge(magnitudes, k + 1)
                if past(k, 2):
                    dve.wait_ge(q_turned, k - 1)
                for u in range(KC):
                    last = dve.tensor_scalar(work_uc[2 + m][:, u, :], work_uc[m][:, u, :], qs[:, 5, u:u + 1],
                                             qs[:, 4, u:u + 1], ALU.subtract, ALU.mult)
                last.then_inc(scaled, 1)

            def levels(k, m, over):
                dve.wait_ge(q_turned, k + 1)
                if past(k, 2):
                    dve.wait_ge(dft_done, k - 1)
                dve.tensor_scalar(qT[m][:, :, :], tokens_of(2 * m), ROUND, ROUND, ALU.add, ALU.subtract
                                  ).then_inc(qT_ready, 1)

            pipeline(dve, NCH, 2, [(0, scale_f), (1, levels)])

            for n, (hl, raw) in enumerate(((wq_hl, w_qv[:, :, 0:C]), (wv_hl, w_qv[:, :, C:]))):
                dve.tensor_copy(hl[:, 0, :, :], raw).then_inc(const_v, 1)
                dve.wait_ge(const_v, 2 * n + 5)
                dve.tensor_tensor(hl[:, 1, :, :], raw, hl[:, 0, :, :], ALU.subtract).then_inc(const_v, 1)

            dve.wait_ge(dft_done, NCH)
            kept = dft[:, :, :]
            s = 1.0 / HW
            n_uns = (NB - NSYM) // 2
            uc, us = NSYM, NSYM + n_uns
            dve.tensor_copy(kept, banks[:, 4:6, 0:3 * NB]).then_inc(coef_steps, 1)
            dve.wait_ge(coef_steps, 1)
            dve.tensor_tensor(kept[:, :, NB:2 * NB], kept[:, :, NB:2 * NB], kept[:, :, 2 * NB:], ALU.add
                              ).then_inc(coef_steps, 1)
            dve.wait_ge(coef_steps, 2)
            dve.tensor_tensor(kept[:, :, 0:NB], kept[:, :, 0:NB], kept[:, :, NB:2 * NB], ALU.add
                              ).then_inc(coef_steps, 1)
            dve.wait_ge(coef_steps, 3)
            dve.memset(coef[:, :, 1, 0:NSYM], 0.0).then_inc(coef_steps, 1)
            for dst, src, scale in ((coef[:, :, 0, 0:1], kept[:, :, 0:1], s),
                                    (coef[:, :, 0, 1:NSYM], kept[:, :, 1:NSYM], 2 * s),
                                    (coef[:, :, 0, uc:NB], kept[:, :, uc:NB], s),
                                    (coef[:, :, 1, uc:us], kept[:, :, us:NB], -s),
                                    (coef[:, :, 1, us:NB], kept[:, :, uc:us], s)):
                dve.tensor_scalar(dst, src, scale, None, ALU.mult).then_inc(coef_steps, 1)
            dve.wait_ge(coef_steps, 9)
            dve.wait_ge(made, MADE)
            dve.tensor_copy(coef16[:, :, :, 0:NB], coef[:, :, :, :]).then_inc(coef_steps, 1)
            dve.tensor_copy(coef16[:, :, :, 2 * PART:2 * PART + NB], coef[:, :, :, :]).then_inc(coef_steps, 1)
            dve.wait_ge(coef_steps, 11)
            dve.tensor_tensor(coef16[:, :, :, PART:PART + NB], coef[:, :, :, :], coef16[:, :, :, 0:NB], ALU.subtract
                              ).then_inc(coef_steps, 1)
            dve.wait_ge(coef_turned, 1)
            dve.tensor_copy(waves[:, :, :, :].rearrange("k r u c -> k (r u c)"),
                            banks[0:3 * PART, 6, 0:256].bitcast(F16)).then_inc(waves_ready, 1)

            def split_root(k, m, over):
                dve.wait_ge(root_ready, k + 1)
                if past(k, 2):
                    dve.wait_ge(queried, k - 1)
                dve.tensor_copy(hi[m][:, :, :], work_uc[2 + m][:, :, :]).then_inc(fq_hi, 1)
                dve.wait_ge(fq_hi, k + 1)
                dve.tensor_tensor(lo[m][:, :, :], work_uc[2 + m][:, :, :], hi[m][:, :, :], ALU.subtract
                                  ).then_inc(fq_lo, 1)

            def query_max(k, m, over):
                dve.wait_ge(queried, k + 1)
                dve.tensor_reduce(m8[:, :].rearrange("p (b t) -> p t b", b=8)[:, bass.ds(k * CT, CT), :],
                                  tokens_of(4 + 2 * m).rearrange("p j (a b) -> p j b a", b=8),
                                  AXX, ALU.max).then_inc(m8_ready, 1)

            pipeline(dve, NCH, 2, [(0, split_root), (1, query_max)])

            dve.wait_ge(m8_ready, NCH)
            dve.wait_ge(blanks, 16 * BLANKS)
            dve.tensor_tensor(gate1[:, 0:PERIOD], m8[:, 0:PERIOD], m8[:, PERIOD:2 * PERIOD], ALU.max
                              ).then_inc(gate_steps, 1)
            dve.wait_ge(gate_steps, 1)
            dve.tensor_tensor(m8[:, 0:PERIOD], gate1[:, 0:PERIOD], m8[:, 2 * PERIOD:], ALU.max).then_inc(gate_steps, 1)
            dve.wait_ge(gate_steps, 2)
            for n in range(3):
                dve.tensor_scalar(gate1[:, n * PERIOD:(n + 1) * PERIOD], m8[:, 0:PERIOD], 1.0, None, ALU.add
                                  ).then_inc(gate_steps, 1)
            dve.wait_ge(gate_steps, 5)

            def gate_value(k, m, over):
                dve.wait_ge(v_done, k + 1)
                if past(k, 2):
                    dve.wait_ge(x1_ready, k - 1)
                mask = gate1[:, 0:E * NT].rearrange("p (b t) -> p t b", b=8)[:, bass.ds(k * CT, CT), :]
                dve.tensor_tensor(work[m % 2][:, :].rearrange("p (j a b) -> p j a b", j=CT, b=8),
                                  tokens_of(2 * (m % 2)).rearrange("p j (a b) -> p j a b", b=8),
                                  mask.unsqueeze(2).broadcast_to([P, CT, C // 8, 8]), ALU.mult).then_inc(gated, 1)

            def residual(k, m, over):
                dve.wait_ge(gated, k + 1)
                chunk = xt[:, bass.ds(k * CT, CT), :]
                dve.tensor_tensor(chunk, chunk, work_jc[m % 2][:, :, :], ALU.add).then_inc(x1_ready, 1)

            def x1_sums(k, m, over):
                hold(dve, x1_ready, k + 1, held)
                if past(k, 1):
                    hold(dve, mv2_done, k * CT, held)
                sums_of(k, 0, bn2_done)

            def x1_gather(k, m, over):
                if past(k, 2):
                    hold(dve, shift2_done, k - 1, held)
                gather(k, m % 2, bn2_done, mv2_done)

            def x1_inverse(k, m, over):
                inverse(k, m % 2, std2_done, rstd2_done, u_ready)

            def x1_offset(k, m, over):
                offset(k, m % 2, rstd2_done, shift2_done)

            def logits_of(m):
                return ut[:, m % 3 * CT:m % 3 * CT + CT, C:NO]

            def route_0(k, m, over):
                dve.wait_ge(logits, k + 1)
                dve.tensor_reduce(top[:, :], gate_out, AXX, ALU.max).then_inc(routed, 1)

            def route_1(k, m, over):
                dve.wait_ge(routed, k * ROUTED + 1)
                dve.tensor_tensor(logits_of(m), gate_out, top[:, :].unsqueeze(2).broadcast_to([P, CT, E]), ALU.subtract
                                  ).then_inc(routed, 1)

            def route_2(k, m, over):
                dve.wait_ge(routed, k * ROUTED + 2)
                dve.tensor_scalar(pick[:, :, :], logits_of(m), 0.0, float(E), ALU.is_lt, ALU.mult).then_inc(routed, 1)

            def route_3(k, m, over):
                dve.wait_ge(routed, k * ROUTED + 3)
                dve.tensor_tensor(pick[:, :, :], pick[:, :, :], iota_e[:, :, :], ALU.add).then_inc(routed, 1)

            def route_4(k, m, over):
                dve.wait_ge(routed, k * ROUTED + 4)
                dve.tensor_reduce(idx[:, :], pick[:, :, :], AXX, ALU.min).then_inc(routed, 1)

            def route_5(k, m, over):
                dve.wait_ge(routed, k * ROUTED + 5)
                dve.tensor_tensor(hot[:, :, 1:].rearrange("p e t -> p t e"), iota_e[:, :, :],
                                  idx[:, :].unsqueeze(2).broadcast_to([P, CT, E]), ALU.is_equal).then_inc(routed, 1)

            def route_6(k, m, over):
                dve.wait_ge(routed, k * ROUTED + 6)
                dve.tensor_tensor_scan(run[:, :, :].rearrange("p e t -> p (e t)"), reset[:, :],
                                       hot[:, :, :].rearrange("p e t -> p (e t)"), 0.0, ALU.mult, ALU.add
                                       ).then_inc(routed, 1)

            def route_7(k, m, over):
                dve.wait_ge(routed, k * ROUTED + 7)
                dve.tensor_copy(hot[:, :, 0:1], run[:, :, CT:]).then_inc(routed, 1)

            def place_0(k, m, over):
                dve.wait_ge(counted, k + 1)
                dve.tensor_tensor(place[:, :, :], banks[:, 7, 0:CT * E].rearrange("p (e t) -> p e t", e=E),
                                  hot[:, :, 1:], ALU.mult).then_inc(placed, 1)

            def place_1(k, m, over):
                dve.wait_ge(placed, k * PLACED + 1)
                dve.tensor_reduce(pos[:, :], place[:, :, :].rearrange("p e t -> p t e"), AXX, ALU.add
                                  ).then_inc(placed, 1)

            def place_2(k, m, over):
                dve.wait_ge(placed, k * PLACED + 2)
                dve.scalar_tensor_tensor(raw_slot[:, :], idx[:, :], float(CAP), pos[:, :], ALU.mult, ALU.add
                                         ).then_inc(placed, 1)
                dve.tensor_scalar(over_cap[:, :], pos[:, :], CAP + 0.5, float(1 << 15), ALU.is_gt, ALU.mult
                                  ).then_inc(placed, 1)

            def place_3(k, m, over):
                mine = ut[:, m % 3 * CT:m % 3 * CT + CT, NO:ROW]
                dve.tensor_copy(mine.bitcast(I32), tok_no[:, bass.ds(k * CT, CT)].unsqueeze(2)).then_inc(placed, 1)
                dve.wait_ge(placed, k * PLACED + 4)
                dve.scalar_tensor_tensor(slot[m % 3][:, :], raw_slot[:, :], -1.0, over_cap[:, :], ALU.add, ALU.add
                                         ).then_inc(placed, 1)

            def x1_sum(j):
                return lambda k, m, over: sums_of(k, j, bn2_done)

            def rest_w(n):
                dve.wait_ge(w_hi, (n + 1) * W_PARTS)
                hl = (w1_hl, w2_hl)[n][0][:, :, :, :].rearrange("p a u c -> p a (u c)")
                dve.tensor_tensor(hl[:, 1, :], w_raw[:, :], hl[:, 0, :], ALU.subtract).then_inc(w_lo, 1)

            def first_w1(k, m, over):
                if isinstance(k, int) and k == NCH - 2:
                    rest_w(0)

            pipeline(dve, NCH, 6, [(5, place_0), (3, x1_inverse), (5, place_1), (3, x1_offset), (5, place_2),
                                   (5, place_3), (5, first_w1),
                                   (2, gate_value), (4, route_0), (2, residual), (4, route_1),
                                   (2, x1_sums), (4, route_2), (2, x1_sum(1)), (4, route_3),
                                   (2, x1_sum(2)), (4, route_4), (2, x1_sum(3)), (4, route_5), (2, x1_gather),
                                   (4, route_6), (4, route_7)])

            def x_rest(s, m):
                dve.wait_ge(xe_hi, s + 1)
                dve.tensor_tensor(x_hl[m % 2][:, 1, :, :], banks[:, 5:7, 0:STEP], x_hl[m % 2][:, 0, :, :], ALU.subtract
                                  ).then_inc(xe_lo, 1)
                dve.wait_ge(exp_done, s + 1)
                if past(s, 1):
                    dve.wait_ge(prob_done, s)
                dve.tensor_reduce(den[:, :], ex[:, :, :], AXX, ALU.add).then_inc(den_done, 1)
                dve.tensor_copy(number[m % PAIR][:, :].unsqueeze(2), rows[m % 3][:, :, NO:ROW].bitcast(I32))
                dve.wait_ge(den_done, s + 1)
                dve.reciprocal(prob[m % PAIR][:, :], den[:, :]).then_inc(prob_done, 1)

            def rest_h(s, m, f):
                g = s * KF + f
                part = h_hl[f % 4]
                dve.wait_ge(h_ready, g + 1)
                dve.tensor_tensor(part[:, 1, :], h32[f % 2][:, :], part[:, 0, :], ALU.subtract).then_inc(h_lo, 1)

            def keep_y1(s, m, i):
                dve.wait_ge(step_done, s + 1)
                if past(s, 1):
                    dve.wait_ge(y_turned, s * 2)
                dve.tensor_scalar(y32[:, 1, :], banks[:, 4, 0:STEP],
                                  b2s[:, bass.ds((i * 2 + m // EXPERT_STEPS) * KC + 1, 1)], None, ALU.add
                                  ).then_inc(y1_kept, 1)

            def guard_y(s, m, r):
                y = y_rows[m % 2][:, 2 * r:2 * r + 2, :].rearrange("p j c -> p (j c)")
                base = s * 12 + 6 * r
                dve.wait_ge(y_scaled, s * 2 + r + 1)
                if past(s, 1) or r:
                    dve.wait_ge(y_guard, base)
                dve.tensor_tensor(y_fix[:, :], y, y, ALU.subtract).then_inc(y_guard, 1)
                dve.wait_ge(y_guard, base + 1)
                dve.tensor_scalar(y_bad[:, :], y_fix[:, :], 0.0, None, ALU.not_equal).then_inc(y_guard, 1)
                dve.wait_ge(y_guard, base + 2)
                dve.tensor_scalar(y_fix[:, :], y, FMAX, None, ALU.is_gt).then_inc(y_guard, 1)
                dve.wait_ge(y_guard, base + 3)
                dve.scalar_tensor_tensor(y_fix[:, :], y, -FMAX, y_fix[:, :], ALU.is_lt, ALU.subtract
                                         ).then_inc(y_guard, 1)
                dve.wait_ge(y_guard, base + 4)
                dve.tensor_scalar(y_fix[:, :], y_fix[:, :], -1e4, None, ALU.mult).then_inc(y_guard, 1)
                hold(dve, y_guard, base + 5, held)
                dve.copy_predicated(y, y_bad[:, :], y_fix[:, :]).then_inc(y_guard, 1)

            rest_w(1)
            x_rest(0, 0)

            def pair(i, first, last):
                for m in range(PAIR):
                    s, before = i * PAIR + m, i * PAIR + (m - 1)
                    some = not (first and m == 0)
                    for f in range(KF):
                        if f == 3 and some:
                            keep_y1(before, m - 1, i)
                        rest_h(s, m, f)
                        if f == 5 and some:
                            guard_y(before, m - 1, 0)
                        if f == 3 and not (last and m == PAIR - 1):
                            x_rest(i * PAIR + (m + 1), m + 1)
                        if f == 7 and some:
                            guard_y(before, m - 1, 1)
                if last:
                    keep_y1(STEPS - 1, PAIR - 1, i)
                    for r in range(2):
                        guard_y(STEPS - 1, PAIR - 1, r)

            pair(0, True, False)
            with dve.Fori(1, PAIRS - 1) as i:
                pair(i, False, False)
            pair(PAIRS - 1, False, True)

            def add_y(k, m, over):
                dve.wait_ge(y_loaded[m], over(6) * 16 + 16)
                if past(k, 3):
                    dve.wait_ge(sum_turned, k - 2)
                dve.tensor_tensor(total[m % 3][:, :, :], xt[:, bass.ds(k * CT, CT), :], y_in[m][:, :, :], ALU.add
                                  ).then_inc(summed, 1)

            pipeline(dve, NCH, 6, [(0, add_y)])

        @block.tensor
        def _(pe):
            pe.wait_ge(made, MADE)

            def to_tokens(bank, src, count=P):
                for j in range(CT):
                    for u in range(KC):
                        last = pe.transpose(tokens_of(bank)[:, j, u * P:(u + 1) * P], src[:, u, j * P:(j + 1) * P],
                                            ident[:, :])
                return last

            def to_planar(bank, src):
                for u in range(KC):
                    for j in range(CT):
                        last = pe.transpose(banks[:, bank + u, j * P:(j + 1) * P], src(j)[:, u * P:(u + 1) * P],
                                            ident[:, :])
                return last

            def turn_x(k, m, over):
                pe.wait_ge(x_loaded[m], over(2) * 16 + 16)
                if past(k, 2):
                    pe.wait_ge(x_kept, k - 1)
                to_tokens(2 * m, work_uc[m]).then_inc(x_turned, 1)

            def turn_f(k, m, over):
                pe.wait_ge(f_ready, k + 1)
                if past(k, 2):
                    pe.wait_ge(f_kept, k - 1)
                to_planar(4 + 2 * m, lambda j: work_jc[2 + m][:, j, :]).then_inc(f_turned, 1)

            pipeline(pe, NCH, 2, [(0, turn_x), (2, turn_f)])

            pe.wait_ge(f_kept, NCH)
            pe.wait_ge(tables_loaded, 16 * TABLES)

            def turn_q(k, m, over):
                pe.wait_ge(scaled, k + 1)
                if past(k, 2):
                    pe.wait_ge(qT_ready, k - 1)
                to_tokens(2 * m, work_uc[2 + m]).then_inc(q_turned, 1)

            def sums(k, m, over):
                pe.wait_ge(qT_ready, k + 1)
                for j in range(CT):
                    for u in range(KC):
                        last = pe.matmul(banks[:, 4 + u, 0:3 * NB], qT[m][:, j, u * P:(u + 1) * P],
                                         basis_f[:, bass.ds(k * CT + j, 1), :].rearrange("p j c -> p (j c)"),
                                         start=isinstance(k, int) and k == 0 and j == 0,
                                         stop=isinstance(k, int) and k == NCH - 1 and j == CT - 1)
                last.then_inc(dft_done, 1)

            pipeline(pe, NCH, 2, [(0, turn_q), (1, sums)])

            pe.wait_ge(coef_steps, 12)
            for r in range(2):
                for u in range(KC):
                    at = (r * KC + u) * P // 2
                    last = pe.transpose(banks[0:3 * PART, 6, at:at + P // 2].bitcast(F16), coef16[:, u, r, :],
                                        ident16[:, :])
            last.then_inc(coef_turned, 1)

            def wave(k, m, over):
                pe.wait_ge(basis_loaded[m], over(2) * 16 + 16)
                for r in range(2):
                    if past(k, 1):
                        pe.wait_ge(squared, k * 2 - 1 + r)
                    for u in range(KC):
                        last = pe.matmul(banks[:, 2 * r + u, :], waves[:, r, u, :], basis_i[m], start=True, stop=True)
                last.then_inc(waved, 1)

            def conv(out_tile, a_hi, a_lo, w, bias):
                n = 0
                for u in range(KC):
                    for a, b in ((a_hi, 0), (a_hi, 1), (a_lo, 0)):
                        pe.matmul(out_tile, a[:, u, :], w[:, b, u, :], start=n == 0, stop=False)
                        n += 1
                return pe.matmul(out_tile, ones2[:, :], bias, start=False, stop=True)

            def query(k, m, over):
                if isinstance(k, int) and k == 0:
                    pe.wait_ge(const_v, CONST_V)
                pe.wait_ge(fq_lo, k + 1)
                if past(k, 2):
                    pe.wait_ge(m8_ready, k - 1)
                for j in range(CT):
                    last = conv(tokens_of(4 + 2 * m)[:, j, :], hi[m][:, :, j * P:(j + 1) * P],
                                lo[m][:, :, j * P:(j + 1) * P], wq_hl, biases[:, 0, :])
                last.then_inc(queried, 1)

            pe.wait_ge(waves_ready, 1)
            pipeline(pe, NCH, 2, [(0, wave), (3, query)])

            pe.wait_ge(squared, 2 * NCH)

            def count(k, m, over):
                pe.wait_ge(routed, k * ROUTED + 7)
                pe.matmul(banks[:, 7, 0:CT * E], tri[:, :], hot[:, :, 1:], start=True, stop=False)
                pe.matmul(banks[:, 7, 0:CT * E], ones_b[:, :], run[:, :, 0:CT], start=False, stop=True
                          ).then_inc(counted, 1)

            def turn_u(k, m, over):
                pe.wait_ge(u_ready, k + 1)
                if past(k, 1):
                    pe.wait_ge(u_kept, k)
                to_planar(4, lambda j: ut[:, m % 3 * CT + j, 0:C]).then_inc(u_turned, 1)

            def gate_logits(k, m, over):
                pe.wait_ge(u_kept, k + 1)
                if past(k, 1):
                    pe.wait_ge(routed, (k - 1) * ROUTED + 2)
                uT = work_uc[2 + m % 2]
                pe.matmul(banks[:, 6, 0:CT * E], ones1[0:1, :], gb_row[:, :], start=True, stop=False)
                for j in range(CT):
                    for u in range(KC):
                        last = pe.matmul(banks[:, 6, j * E:(j + 1) * E], uT[:, u, j * P:(j + 1) * P], gate_col[:, u, :],
                                         start=False, stop=(j, u) == (CT - 1, KC - 1))
                last.then_inc(logits, 1)

            def value(k, m, tiles):
                for j in tiles:
                    last = conv(tokens_of(2 * (m % 2))[:, j, :], hi[m % 2][:, :, j * P:(j + 1) * P],
                                lo[m % 2][:, :, j * P:(j + 1) * P], wv_hl, biases[:, 1, :])
                return last

            def value_first(k, m, over):
                pe.wait_ge(v_lo, k + 1)
                if past(k, 2):
                    pe.wait_ge(gated, k - 1)
                value(k, m, (0, 1))

            def value_last(k, m, over):
                value(k, m, (2, 3)).then_inc(v_done, 1)

            pipeline(pe, NCH, 6, [(1, value_first), (3, turn_u), (1, value_last), (4, count), (3, gate_logits)])

            def turn_rows(s, m, loads):
                pe.wait_ge(rows_loaded[m % 3], loads)
                if past(s, 1):
                    pe.wait_ge(xe_lo, s)
                for u in range(KC):
                    for j in range(SJ):
                        last = pe.transpose(banks[:, 5 + u, j * SP_:(j + 1) * SP_],
                                            rows[m % 3][:, j, u * P:(u + 1) * P], ident[0:SP_, 0:SP_])
                last.then_inc(rows_turned, 1)

            def up(s, m, f, i):
                g = s * KF + f
                b = m // EXPERT_STEPS
                if f == 0:
                    pe.wait_ge(xe_lo, s + 1)
                    pe.wait_ge(w_lo, (i * 2 + b) * 2 + 1)
                if past(s, 1) or f >= 3:
                    pe.wait_ge(h_ready, g - 2)
                o = banks[:, (m * KF + f) % 3, 0:STEP]
                n = 0
                for u in range(KC):
                    for wp, xp in ((0, 0), (0, 1), (1, 0)):
                        last = pe.matmul(o, w1_hl[b][:, wp, u, f * P:(f + 1) * P], x_hl[m % 2][:, xp, u, :],
                                         start=n == 0, stop=n == 5)
                        n += 1
                last.then_inc(up_done, 1)

            def down(s, m, f, i):
                g = s * KF + f
                b = m // EXPERT_STEPS % 2
                part = h_hl[f % 4]
                pe.wait_ge(h_lo, g + 1)
                if f == 0:
                    pe.wait_ge(w_lo, (i * 2 + b) * 2 + 2)
                    if past(s, 1):
                        pe.wait_ge(y0_kept, s)
                        pe.wait_ge(y1_kept, s)
                for u in range(KC):
                    for wp, hp in ((0, 0), (0, 1), (1, 0)):
                        last = pe.matmul(banks[:, 3 + u, 0:STEP], w2_hl[b][:, wp, f, u * P:(u + 1) * P], part[:, hp, :],
                                         start=f == 0 and wp + hp == 0, stop=f == KF - 1 and wp == 1)
                last.then_inc(down_done, 1)
                if f == KF - 1:
                    pe.wait_ge(down_done, g + 1)
                    pe.sem_inc(step_done, 1)

            def turn_y(s, m, r):
                if r == 0:
                    pe.wait_ge(y0_kept, s + 1)
                    pe.wait_ge(y1_kept, s + 1)
                if past(s, 1) or r:
                    pe.wait_ge(y_scaled, s * 2 + r)
                for jj in range(2):
                    for u in range(KC):
                        j = 2 * r + jj
                        last = pe.transpose(banks[0:SP_, 7, jj * C + u * P:jj * C + (u + 1) * P],
                                            y32[:, u, j * SP_:(j + 1) * SP_], ident[:, :])
                last.then_inc(y_turned, 1)

            def warm(times):
                with pe.Fori(0, times):
                    for _ in range(4):
                        pe.matmul(banks[:, 7, 0:2 * P], one_half[:, 0:P], one_half[:, :], start=True, stop=True)

            one_half = ident[:, :].bitcast(BF16)
            pe.wait_ge(placed, PLACED * NCH)
            warm(WARM0)
            turn_rows(0, 0, 16)
            warm(WARM1)

            def pair(i, first, last):
                for m in range(PAIR):
                    for f in range(KF):
                        up(i * PAIR + m, m, f, i)
                        if not (first and m == 0 and f < 3):
                            dm, df = divmod(m * KF + f - 3, KF)
                            down(i * PAIR + dm, dm, df, i)
                        if f in (4, 6) and not (first and m == 0):
                            turn_y(i * PAIR + (m - 1), m - 1, (f - 4) // 2)
                        if f == 2 and not (last and m == PAIR - 1):
                            turn_rows(i * PAIR + (m + 1), m + 1, i * 32 + ((m + 1) // 3 + 1) * 16)
                if last:
                    for f in (KF - 3, KF - 2, KF - 1):
                        down(STEPS - 1, PAIR - 1, f, i)
                    for r in range(2):
                        turn_y(STEPS - 1, PAIR - 1, r)

            pair(0, True, False)
            with pe.Fori(1, PAIRS - 1) as i:
                pair(i, False, False)
            pair(PAIRS - 1, False, True)

            def turn_sum(k, m, over):
                pe.wait_ge(summed, k + 1)
                if past(k, 3):
                    pe.wait_ge(sum_kept, k - 2)
                to_planar(2 * m, lambda j: total[m][:, j, :]).then_inc(sum_turned, 1)

            pipeline(pe, NCH, 3, [(0, turn_sum)])


def waves_tables():
    mirrored = [(0, 1), (1, 0), (1, 1), (1, -1)]
    alone = [(-2, v) for v in (-2, -1, 0, 1)] + [(u, -2) for u in (-1, 0, 1)]
    h, w = np.divmod(np.arange(HW), W)

    def angle(u, v):
        return 2 * np.pi * ((u * h + v * w) % H) / H

    rows = [np.ones(HW)]
    for some in (mirrored, alone):
        rows += [np.cos(angle(u, v)) for u, v in some] + [np.sin(angle(u, v)) for u, v in some]
    table = np.stack(rows)

    def parts(dtype, n):
        left, out = table.copy(), []
        for _ in range(n):
            out.append(left.astype(dtype))
            left = left - out[-1].astype(np.float64)
        return out

    bf16 = mybir.dt.np(BF16)
    fwd = np.concatenate(parts(bf16, 3), 0)
    fwd = np.ascontiguousarray(fwd.T.reshape(NT, P, 3 * NB).transpose(1, 0, 2))
    hi16, lo16 = parts(np.float16, 2)
    inv = np.zeros((3 * PART, HW), np.float16)
    for n, rows16 in enumerate((hi16, hi16, lo16)):
        inv[n * PART:n * PART + NB] = rows16
    return fwd, inv


def kernel(**inputs):
    import concourse.bacc as _bacc
    from concourse.bass_utils import run_bass_kernel_spmd as _run

    a = {n: np.asarray(v) for n, v in inputs.items()}
    fwd, inv = waves_tables()
    f, c = "L0_ffn_", "L0_conv_"
    arrays = {
        "x": a["x"].reshape(C, HW),
        "wT": np.concatenate([a[c + "Wq"].T, a[c + "Wv"].T], 1),
        "b_qv": np.tile(np.stack([a[c + "bq"], a[c + "bv"]])[None], (2, 1, 1)),
        "gate_w": a[f + "gate_w"], "gate_b": np.tile(a[f + "gate_b"], CT).reshape(1, CT * E),
        "w1": a[f + "w1"], "w2": a[f + "w2"],
        "b12T": np.concatenate([a[f + "b1"].reshape(E, KF, P).transpose(2, 0, 1).reshape(P, E * KF),
                                a[f + "b2"].reshape(E, KC, P).transpose(2, 0, 1).reshape(P, E * KC)], 1),
        "fwd": fwd, "inv": inv,
    }
    arrays = {n: np.ascontiguousarray(v) for n, v in arrays.items()}
    nc = _bacc.Bacc("TRN2", target_bir_lowering=False, num_devices=1)
    args = [nc.dram_tensor("in_" + n, v.shape, mybir.dt.from_np(v.dtype), kind="ExternalInput").ap()
            for n, v in arrays.items()]
    out = nc.dram_tensor("out_0_dram", (C, HW), F32, kind="ExternalOutput").ap()
    program(nc, *args, out)
    r = _run(nc, [{"in_" + n: v for n, v in arrays.items()}], core_ids=[0])
    return r.results[0]["out_0_dram"].reshape(1, C, H, W)
```
